# Optimizing a Trainium2 kernel written in Bass

```python
import numpy as np
import jax
import jax.numpy as jnp

def _softmax(x, axis=-1):
    return jax.nn.softmax(x, axis=axis)

def _gelu(x):
    return jax.nn.gelu(x, approximate=True)

def _silu(x):
    return jax.nn.silu(x)

def _sigmoid(x):
    return jax.nn.sigmoid(x)

def _layernorm(x, axis=-1, eps=1e-05):
    m = jnp.mean(x, axis=axis, keepdims=True)
    v = jnp.var(x, axis=axis, keepdims=True)
    return (x - m) / jnp.sqrt(v + eps)

def _scatter_add(tgt, idx, src, axis=0):
    return tgt.at[idx].add(src)

def _segment_sum(src, seg, n):
    return jax.ops.segment_sum(src, seg, n)
kernel_name = 'mk_adaln_d1_jaxref_r4_600426'

def setup_inputs(seed: int=0):
    np.random.seed(seed)
    _w = jnp.asarray

    def _L0_attn_setup():
        import jax, jax.numpy as jnp
        import numpy as np
        D_MODEL = 256
        N_HEADS = 16
        D_HEAD = 64
        B, S = (8, 256)
        EPS = 1.1920929e-07
        key = jax.random.key(seed)
        k1, k2, k3 = jax.random.split(key, 3)
        x = jax.random.normal(k1, (B, S, D_MODEL), dtype=jnp.float32)
        W_qkv = jax.random.normal(k2, (3 * N_HEADS * D_HEAD, D_MODEL), dtype=jnp.float32) * 0.02
        b_qkv = jnp.zeros((3 * N_HEADS * D_HEAD,), dtype=jnp.float32)
        W_o = jax.random.normal(k3, (D_MODEL, N_HEADS * D_HEAD), dtype=jnp.float32) * 0.02
        b_o = jnp.zeros((D_MODEL,), dtype=jnp.float32)
        return {'x': x, 'W_qkv': W_qkv, 'b_qkv': b_qkv, 'W_o': W_o, 'b_o': b_o}
    _L0_attn_in = _L0_attn_setup()

    def _L0_ffn_setup():
        import jax, jax.numpy as jnp
        import numpy as np
        B, S, D, H, E = (8, 512, 256, 1024, 16)
        key = jax.random.key(seed)
        ks = jax.random.split(key, 4)
        sd = 1.0 / np.sqrt(D).astype(np.float32)
        sh = 1.0 / np.sqrt(H).astype(np.float32)
        return {'x': jax.random.normal(ks[0], (B, S, D), jnp.float32), 'Wg': jax.random.normal(ks[1], (D, E), jnp.float32) * sd, 'bg': jnp.zeros((E,), jnp.float32), 'W1': jax.random.normal(ks[2], (E, D, H), jnp.float32) * sd, 'b1': jnp.zeros((E, H), jnp.float32), 'W2': jax.random.normal(ks[3], (E, H, D), jnp.float32) * sh, 'b2': jnp.zeros((E, D), jnp.float32)}
    _L0_ffn_in = _L0_ffn_setup()
    _L0_c = _w((lambda *s: np.random.randn(*s).astype(np.float32) * 0.05)(4, 256))
    _L0_wmod = _w((lambda *s: np.random.randn(*s).astype(np.float32) * 0.05)(256, 6 * 256) * 256 ** (-0.5))
    _d = {'L0_attn_x': _L0_attn_in['x'], 'L0_attn_W_qkv': _L0_attn_in['W_qkv'], 'L0_attn_b_qkv': _L0_attn_in['b_qkv'], 'L0_attn_W_o': _L0_attn_in['W_o'], 'L0_attn_b_o': _L0_attn_in['b_o'], 'L0_ffn_Wg': _L0_ffn_in['Wg'], 'L0_ffn_bg': _L0_ffn_in['bg'], 'L0_ffn_W1': _L0_ffn_in['W1'], 'L0_ffn_b1': _L0_ffn_in['b1'], 'L0_ffn_W2': _L0_ffn_in['W2'], 'L0_ffn_b2': _L0_ffn_in['b2'], 'L0_c': _L0_c, 'L0_wmod': _L0_wmod}
    _x0 = _d['L0_attn_x']
    _d['L0_attn_x'] = jax.random.normal(jax.random.fold_in(jax.random.key(seed), 1), (4, 1024, 256), dtype=_x0.dtype)
    del _x0
    return _d

def reference(L0_attn_x, L0_attn_W_qkv, L0_attn_b_qkv, L0_attn_W_o, L0_attn_b_o, L0_ffn_Wg, L0_ffn_bg, L0_ffn_W1, L0_ffn_b1, L0_ffn_W2, L0_ffn_b2, L0_c, L0_wmod):

    def _L0_attn_ref(x, W_qkv, b_qkv, W_o, b_o):
        import jax, jax.numpy as jnp
        import numpy as np
        D_MODEL = 256
        N_HEADS = 16
        D_HEAD = 64
        B, S = (8, 256)
        EPS = 1.1920929e-07
        normed = x * jax.lax.rsqrt(jnp.mean(x * x, axis=-1, keepdims=True) + EPS)
        qkv = normed @ W_qkv.T + b_qkv
        qkv = qkv.reshape(*qkv.shape[:-1], N_HEADS, D_HEAD, 3)
        q, k, v = (qkv[..., 0], qkv[..., 1], qkv[..., 2])
        scores = jnp.einsum('bqhd,bkhd->bhqk', q, k)
        seq = x.shape[-2]
        causal_mask = jnp.triu(jnp.ones((seq, seq), dtype=bool), k=1)
        scores = jnp.where(causal_mask, -jnp.inf, scores)
        attn = jax.nn.softmax(scores, axis=-2)
        z = jnp.einsum('bhqk,bkhd->bqhd', attn, v)
        z = z.reshape(*z.shape[:-2], N_HEADS * D_HEAD)
        return z @ W_o.T + b_o

    def _L0_ffn_ref(x, Wg, bg, W1, b1, W2, b2):
        import jax, jax.numpy as jnp
        import numpy as np
        B, S, D, H, E = (8, 512, 256, 1024, 16)
        d = x.shape[-1]
        xf = x.reshape(-1, d)
        n_tok = xf.shape[0]
        n_exp = Wg.shape[1]
        cap = -(-n_tok // n_exp)
        score = jax.nn.softmax(xf @ Wg + bg, axis=-1)
        gate = jnp.max(score, axis=-1)
        idx = jnp.argmax(score, axis=-1)
        onehot = jax.nn.one_hot(idx, n_exp, dtype=jnp.int32)
        pos = jnp.sum((jnp.cumsum(onehot, axis=0) - 1) * onehot, axis=-1)
        keep = pos < cap
        safe_pos = jnp.where(keep, pos, cap - 1)
        buf = jnp.zeros((n_exp, cap, d), x.dtype).at[idx, safe_pos].add(jnp.where(keep[:, None], xf, 0.0))
        h = jax.nn.relu(jnp.einsum('ecd,edh->ech', buf, W1) + b1[:, None, :])
        y = jnp.einsum('ech,ehd->ecd', h, W2) + b2[:, None, :]
        out = y[idx, safe_pos] * gate[:, None]
        out = jnp.where(keep[:, None], out, 0.0)
        return out.reshape(x.shape)
    x = L0_attn_x
    mod = (_silu(L0_c) @ L0_wmod).reshape(L0_c.shape[0], 6, 1, -1)
    sa, ca, ga, sb, cb, gb = (mod[:, 0], mod[:, 1], mod[:, 2], mod[:, 3], mod[:, 4], mod[:, 5])
    ga = (2 * (ga >= 0) - 1) * jnp.maximum(jnp.abs(ga), 0.25)
    gb = (2 * (gb >= 0) - 1) * jnp.maximum(jnp.abs(gb), 0.25)
    h = _layernorm(x, axis=-1) * (1 + ca) + sa
    x = x + ga * _L0_attn_ref(h, L0_attn_W_qkv, L0_attn_b_qkv, L0_attn_W_o, L0_attn_b_o)
    h = _layernorm(x, axis=-1) * (1 + cb) + sb
    x = x + gb * _L0_ffn_ref(h, L0_ffn_Wg, L0_ffn_bg, L0_ffn_W1, L0_ffn_b1, L0_ffn_W2, L0_ffn_b2)
    return x

_drawn_inputs = setup_inputs


def setup_inputs(seed=0):
    import zlib

    import numpy as np

    out = dict(_drawn_inputs(seed))
    spreads = {'L0_attn_b_qkv': (0.0, 0.333),
     'L0_attn_b_o': (0.0, 0.296),
     'L0_ffn_bg': (0.0, 0.501),
     'L0_ffn_b1': (0.0, 0.8),
     'L0_ffn_b2': (0.0, 0.8)}
    factors = {'L0_attn_W_qkv': 4.907}
    for name, (base, spread) in spreads.items():
        noise = np.random.default_rng([zlib.crc32(name.encode()), seed]).standard_normal(out[name].shape)
        drawn = base * np.exp(spread * noise) if base else spread * noise
        out[name] = jnp.asarray(drawn.astype(out[name].dtype))
    for name, factor in factors.items():
        out[name] = (out[name] * factor).astype(out[name].dtype)
    return out
```

```python
from contextlib import ExitStack

import concourse.bass as bass
from concourse import mybir

P = 128
B, S, D = 4, 1024, 256
H, DH = 16, 64
PAIRS = H // 2
NG = B * PAIRS
TPB = S // P
NT = B * TPB
NC = D // P
NE, HID = 16, 1024
NM = HID // P
CAP = B * S // NE
HALF = 512
LAG = PAIRS + 1
QKV = 3 * P
WROW = NC * QKV + 2
LN_EPS = 1e-5
RMS_EPS = 1.1920929e-07
BIG = 3.0e38
FAR = float(1 << 20)

ALU = mybir.AluOpType
ACT = mybir.ActivationFunctionType
AX = mybir.AxisListType
F32 = mybir.dt.float32
F32R = mybir.dt.float32r
U32 = mybir.dt.uint32

ONE = 1

SA, CA, GA, SB, CB, GB = range(6)

RISES = {
    "scores": dict(att=TPB), "negmax": dict(att=TPB), "expd": dict(att=TPB), "vscaled": dict(att=TPB),
    "rowinv": dict(att=TPB), "pv": dict(att=TPB), "zevac": dict(att=1),
    "auxa": dict(proj=3, post=3), "auxb": dict(proj=3, ln=1),
    "hi": dict(proj=4), "nbk": dict(proj=1),
    "xn": dict(ln=1), "lnve": dict(ln=1), "rstd": dict(ln=1), "h": dict(ln=1), "ss": dict(ln=1), "ms": dict(ln=1),
    "rr": dict(ln=1), "hn": dict(ln=1),
    "x1": dict(post=1), "pve": dict(post=1), "prstd": dict(post=1), "xn2": dict(post=1),
    "h2": dict(post=1),
    "dlink": dict(ln=2, post=2), "plink": dict(ln=1, post=2),
}


class Step:

    def __init__(self, seg, b, j, pp, before, since):
        self.seg, self.b, self.j, self.pp, self.before, self.since = seg, b, j, pp, before, since
        self.i = 2 * j + pp
        self.g = b * PAIRS - 1 + self.i
        self.tile = self.g - LAG
        self.att_par, self.proj_par = 1 - pp, pp

    def has(self, part):
        return part in self.seg

    def n(self, name):
        per = sum(v for k, v in RISES[name].items() if k in self.seg)
        return self.before[name] + per * self.since

    def of(self, name, k):
        return self.n(name) + k


SEGS = [
    (-1, 0, 4, (0, 1), ("ln",)),
    (0, 0, 1, (0,), ("proj", "ln")),
    (0, 0, 1, (1,), ("att", "proj", "ln")),
    (0, 1, 4, (0, 1), ("att", "proj", "ln")),
    (1, 0, 1, (0, 1), ("att", "proj", "ln")),
    (1, 1, 4, (0, 1), ("att", "proj", "ln", "post")),
    (2, 0, 4, (0, 1), ("att", "proj", "ln", "post")),
    (3, 0, 4, (0, 1), ("att", "proj", "post")),
    (4, 0, 1, (0,), ("att", "post")),
    (4, 0, 1, (1,), ("post",)),
    (4, 1, 5, (0, 1), ("post",)),
]


def rises_before(k):
    done = {name: ONE for name in RISES}
    for b, j0, j1, halves, parts in SEGS[:k]:
        steps = (j1 - j0) * len(halves)
        for name, per in RISES.items():
            done[name] += steps * sum(v for part, v in per.items() if part in parts)
    return done


def run_steps(eng, body):
    for k, (b, j0, j1, halves, parts) in enumerate(SEGS):
        before = rises_before(k)
        if j1 - j0 == 1:
            for n, pp in enumerate(halves):
                body(Step(parts, b, j0, pp, before, n))
        else:
            with eng.Fori(j0, j1) as j:
                for pp in halves:
                    body(Step(parts, b, j, pp, before, 2 * (j - j0) + pp))


TOTAL = rises_before(len(SEGS))


def start_counters(eng, sems):
    for x in sems:
        eng.sem_inc(x, ONE)


def settle(eng, passed):
    eng.sem_inc(passed, 1)


def qk_count(st):
    return 8 * 16 * (st.b * PAIRS // 2 + st.j + st.pp)


def zx_count(st):
    return 32 * (st.b * PAIRS // 2 + st.j - (LAG + 1) // 2 + 1)


def adaln_block(nc, x_d, wqkv_d, bv_d, wo_d, bo_d, wg_d, bg_d, w1_d, b1_d, w2_d, b2_d, c_d, wmod_d, out_d):
    keep = ExitStack()
    with keep:
        def dram(name, shape, dt=F32):
            return nc.dram_tensor(name, shape, dt, kind="Internal").ap()

        def sb(name, shape, dt=F32, stack=keep):
            return stack.enter_context(nc.sbuf_tensor(name, shape, dt))

        def sem(name):
            return keep.enter_context(nc.semaphore(name))

        mod_s = dram("mod_s", [B, 6 * D])
        z_s = dram("z_s", [NG, P, S])
        x1_s = dram("x1_s", [NT, P, D])
        h2_s = dram("h2_s", [NT, P, D])
        slots_s = dram("slots_s", [NE * CAP, D])
        y_s = dram("y_s", [NE * CAP, D])

        ident = sb("ident", [P, P])
        modB = sb("modB", [P, B, 6, D])
        logits = sb("logits", [P, NT, NE])
        slot_u = sb("slot_u", [P, NT], U32)
        gates = sb("gates", [P, NT])
        mhalf = sb("mhalf", [P, 1])

        woT = sb("woT", [P, PAIRS, D])
        boB = sb("boB", [P, D])
        wg = sb("wg", [P, NC, NE])
        bgB = sb("bgB", [P, NE])
        zt = sb("zt", [P, 2, PAIRS, P])
        xp = sb("xp", [P, 2, D])
        pt = sb("pt", [P, D])
        pt2 = sb("pt2", [P, D])
        x1 = sb("x1", [P, 2, D])
        xn2 = sb("xn2", [P, D])
        h2a = sb("h2a", [P, D])
        h2 = sb("h2", [P, 2, D])
        h2T = sb("h2T", [P, NC, P])
        pst = sb("pst", [P, 6])
        pmv = sb("pmv", [P, 2])
        pve = sb("pve", [P, 1])
        prs = sb("prs", [P, 1])

        att = ExitStack()
        E = sb("E", [P, 2, 2, S], stack=att)
        QS = sb("QS", [P, 2, 2, S], F32R, stack=att)
        KS = sb("KS", [P, 2, 2, 2, S], F32R, stack=att)
        XQ = sb("XQ", [P, 2, S], F32R, stack=att)
        XK = sb("XK", [P, 2, S], F32R, stack=att)
        V = sb("V", [P, 2, TPB, P], stack=att)
        vs = sb("vs", [P, 2, P], stack=att)
        rs = sb("rs", [P, TPB, 2], stack=att)
        ri = sb("ri", [P, 2, 2], stack=att)
        nm = sb("nm", [P, 2, TPB], stack=att)
        mask = sb("mask", [P, S], stack=att)
        hT = sb("hT", [P, 2, NC, S], stack=att)
        W = sb("W", [P, 2, WROW], stack=att)
        nbk = sb("nbk", [P, 1], stack=att)
        bvB = sb("bvB", [P, PAIRS * P], stack=att)
        zs = sb("zs", [P, S], stack=att)
        xln = sb("xln", [P, 2, D], stack=att)
        xnb = sb("xnb", [P, D], stack=att)
        ha = sb("ha", [P, D], stack=att)
        hb = sb("hb", [P, D], stack=att)
        hsq = sb("hsq", [P, D], stack=att)
        hn = sb("hn", [P, D], stack=att)
        lst = sb("lst", [P, 6], stack=att)
        lmv = sb("lmv", [P, 2], stack=att)
        lve = sb("lve", [P, 1], stack=att)
        lrs = sb("lrs", [P, 1], stack=att)
        lss = sb("lss", [P, 1], stack=att)
        lms = sb("lms", [P, 1], stack=att)
        lrr = sb("lrr", [P, 1], stack=att)
        wmod = E[:, 0, :, :].rearrange("p a b -> p (a b)")
        wmod2 = E[:, 1, :, :].rearrange("p a b -> p (a b)")
        cT = sb("cT", [P, NC * B], stack=att)
        ec = sb("ec", [P, NC * B], stack=att)
        sc = sb("sc", [P, NC * B], stack=att)
        modr = sb("modr", [B, 6 * D], stack=att)
        sgn = sb("sgn", [B, 2, D], stack=att)
        att.close()

        moe = ExitStack()
        keep.enter_context(moe)
        W1 = sb("W1", [P, 2, NC, HID])
        W2 = sb("W2", [P, 2, NM, D])
        b1t = sb("b1t", [P, 2, NM])
        b2B = sb("b2B", [P, 2, D])
        zero = sb("zero", [P, 2 * D])
        tri = sb("tri", [P, P])
        ones = sb("ones", [P, P])
        revj = sb("revj", [P, NE])
        ebase = sb("ebase", [P, NE])
        ra = sb("ra", [P, NT, NE])
        rb = sb("rb", [P, NT, NE])
        rc = sb("rc", [P, NT, NE])
        oh = sb("oh", [P, NT, NE])
        base = sb("base", [P, NT, NE])
        r1 = sb("r1", [P, NT])
        r2 = sb("r2", [P, NT])
        r3 = sb("r3", [P, NT])
        r4 = sb("r4", [P, NT])
        keepm = sb("keepm", [P, NT])
        hs = sb("hs", [P, 4, D])
        idx = sb("idx", [P, 4], U32)
        gcol = sb("gcol", [P, 4])
        xb = sb("xb", [P, 2, 2, D])
        bT = sb("bT", [P, 2, NC, CAP])
        hh = sb("hh", [P, NM, CAP])
        yb = sb("yb", [P, 2, 2, D])
        gat = sb("gat", [P, 4, D])
        fx = sb("fx", [P, 4, D])
        ft = sb("ft", [P, 2, D])
        fo = sb("fo", [P, 4, D])

        SC = [keep.enter_context(nc.psum_tensor(f"SC{h}", [P, S], F32)) for h in range(2)]
        Z = keep.enter_context(nc.psum_tensor("Z", [P, S], F32))
        XA = keep.enter_context(nc.psum_tensor("XA", [P, HALF], F32))
        XB = keep.enter_context(nc.psum_tensor("XB", [P, HALF], F32))

        names = [n for n in RISES if n not in ("scores", "negmax", "expd")]
        s = {n: sem("s_" + n) for n in names}
        scores_done = [sem(f"scores_done{h}") for h in range(2)]
        negmax_done = [sem(f"negmax_done{h}") for h in range(2)]
        exp_done = [sem(f"exp_done{h}") for h in range(2)]
        auxa_full, auxa_free = s["auxa"], sem("auxa_free")
        auxb_full, auxb_free = s["auxb"], sem("auxb_free")
        w_in = [sem(f"w_in{k}") for k in range(2)]
        qk_in = [sem(f"qk_in{k}") for k in range(2)]
        xln_in = [sem(f"xln_in{k}") for k in range(2)]
        zx_in = [sem(f"zx_in{k}") for k in range(2)]
        z_out = sem("z_out")
        post_out = [sem(f"post_out{k}") for k in range(2)]
        const_in = sem("const_in")
        mod_in = sem("mod_in")
        mod_out = sem("mod_out")
        modb_in = sem("modb_in")
        consts = sem("consts")
        c_exp = sem("c_exp")
        setup = sem("setup")
        silu_done = sem("silu_done")
        mod_mm = sem("mod_mm")
        mod_rows = sem("mod_rows")

        zeroed = sem("zeroed")
        moe_const = sem("moe_const")
        route = sem("route")
        route_exp0 = sem("route_exp0")
        route_exp = sem("route_exp")
        onehot = sem("onehot")
        prefix_mm = sem("prefix_mm")
        routed = sem("routed")
        hs_in = [sem(f"hs_in{k}") for k in range(4)]
        idx_ok = sem("idx_ok")
        scattered = [sem(f"scattered{k}") for k in range(4)]
        we_in = [sem(f"we_in{k}") for k in range(2)]
        xb_in = [sem(f"xb_in{k}") for k in range(2)]
        xbT_mm = sem("xbT_mm")
        bT_done = sem("bT_done")
        hid_mm = [sem(f"hid_mm{m}") for m in range(4)]
        hid_done = [sem(f"hid_done{m}") for m in range(4)]
        y_mm = sem("y_mm")
        y_done = sem("y_done")
        y_out = [sem(f"y_out{k}") for k in range(2)]
        gat_clear = sem("gat_clear")
        gat_in = [sem(f"gat_in{k}") for k in range(4)]
        fx_in = [sem(f"fx_in{k}") for k in range(4)]
        scaled = sem("scaled")
        summed = sem("summed")
        out_done = [sem(f"out_done{k}") for k in range(4)]

        sp_passed, dve_passed, pool_passed = sem("sp_passed"), sem("dve_passed"), sem("pool_passed")

        block = keep.enter_context(nc.Block())

        @block.sync
        def _(sp):
            start_counters(sp, [*post_out, *y_out, *out_done])
            sp.dma_start(cT[:, :], c_d).then_inc(mod_in, 16)
            sp.dma_start(wmod[:, 0:6 * D], wmod_d[0]).then_inc(mod_in, 16)
            sp.dma_start(wmod2[:, 0:6 * D], wmod_d[1]).then_inc(mod_in, 16)
            sp.dma_start(woT[:, :, :], wo_d).then_inc(const_in, 16)
            sp.dma_start(boB[:, :], bo_d.broadcast_to([P, D])).then_inc(const_in, 16)
            sp.dma_start(wg[:, :, :], wg_d).then_inc(const_in, 16)
            sp.dma_start(bgB[:, :], bg_d.broadcast_to([P, NE])).then_inc(const_in, 16)
            sp.dma_start(bvB[:, :], bv_d.broadcast_to([P, PAIRS * P])).then_inc(const_in, 16)
            sp.wait_ge(mod_rows, 6)
            sp.dma_start(mod_s, modr[:, :]).then_inc(mod_out, 16)
            sp.wait_ge(mod_out, 16)
            sp.dma_start(modB[:, :, :, :].rearrange("p b k d -> p (b k d)"),
                         mod_s.rearrange("b n -> (b n)").unsqueeze(0).broadcast_to([P, B * 6 * D])).then_inc(modb_in, 16)

            def step(st):
                g = st.g
                if st.has("proj"):
                    sp.wait_ge(auxa_free, st.n("auxa"))
                    settle(sp, sp_passed)
                    sp.wait_ge(auxb_free, st.n("auxb"))
                    settle(sp, sp_passed)
                    sp.dma_start(W[:, st.pp, :], wqkv_d[st.i]).then_inc(w_in[st.pp], 16)
                if st.has("ln"):
                    sp.wait_ge(s["xn"], st.n("xn"))
                    settle(sp, sp_passed)
                    sp.dma_start(xln[:, st.pp, :], x_d[(st.b + 1) * TPB + st.i]).then_inc(xln_in[st.pp], 16)
                if st.has("post"):
                    t = st.tile
                    bt = t // TPB
                    tt = t % TPB
                    sp.wait_ge(z_out, 16 * (g - 1 if st.has("att") else NG))
                    settle(sp, sp_passed)
                    sp.wait_ge(auxa_free, st.n("auxa"))
                    settle(sp, sp_passed)
                    sp.dma_start(zt[:, st.pp, :, :],
                                 z_s[bass.ds(bt * PAIRS, PAIRS), :, bass.ds(tt * P, P)].rearrange("c p t -> p c t")).then_inc(zx_in[st.pp], 16)
                    sp.wait_ge(s["x1"], st.n("x1"))
                    settle(sp, sp_passed)
                    sp.dma_start(xp[:, st.pp, :], x_d[t]).then_inc(zx_in[st.pp], 16)
                if st.has("proj"):
                    sp.wait_ge(s["hi"], st.of("hi", 4))
                    settle(sp, sp_passed)
                    sp.wait_ge(auxa_free, st.of("auxa", 2 + st.has("post")))
                    settle(sp, sp_passed)
                    sp.wait_ge(auxb_free, st.of("auxb", 2))
                    settle(sp, sp_passed)
                    sp.wait_ge(scores_done[1], st.n("scores"))
                    settle(sp, sp_passed)
                    for h in range(2):
                        rows = slice(DH * h, DH * h + DH)
                        for part in range(2):
                            to = slice(DH * part, DH * part + DH)
                            sp.dma_start(QS[to, st.proj_par, h, :].bitcast(F32), XQ[rows, part, :].bitcast(F32)).then_inc(qk_in[st.proj_par], 16)
                            sp.dma_start(KS[to, st.proj_par, h, :, :].bitcast(F32), XK[rows, :, :].bitcast(F32)).then_inc(qk_in[st.proj_par], 16)
                if st.has("att"):
                    sp.wait_ge(s["zevac"], st.of("zevac", 1))
                    settle(sp, sp_passed)
                    sp.dma_start(z_s[g], zs[:, :]).then_inc(z_out, 16)
                if st.has("post"):
                    sp.wait_ge(s["x1"], st.of("x1", 1))
                    settle(sp, sp_passed)
                    sp.dma_start(x1_s[t], x1[:, st.pp, :]).then_inc(post_out[st.pp], 16)
                    sp.wait_ge(s["h2"], st.of("h2", 1))
                    settle(sp, sp_passed)
                    sp.dma_start(h2_s[t], h2[:, st.pp, :]).then_inc(post_out[st.pp], 16)

            run_steps(sp, step)

            sp.wait_ge(s["pv"], TOTAL["pv"])
            settle(sp, sp_passed)
            sp.wait_ge(s["zevac"], TOTAL["zevac"])
            settle(sp, sp_passed)
            sp.wait_ge(z_out, 16 * NG)
            settle(sp, sp_passed)

            def load_expert(e, pp):
                sp.dma_start(W1[:, pp, :, :], w1_d[e].rearrange("(c p) n -> p c n", p=P)).then_inc(we_in[pp], 16)
                sp.dma_start(W2[:, pp, :, :], w2_d[e].rearrange("(m p) n -> p m n", p=P)).then_inc(we_in[pp], 16)
                sp.dma_start(b1t[:, pp, :], b1_d[e]).then_inc(we_in[pp], 16)
                sp.dma_start(b2B[:, pp, :], b2_d[e].unsqueeze(0).broadcast_to([P, D])).then_inc(we_in[pp], 16)

            def load_slots(e, pp):
                sp.dma_start(xb[:, pp, :, :], slots_s[bass.ds(e * CAP, CAP), :].rearrange("(i p) d -> p i d", p=P)).then_inc(xb_in[pp], 16)

            def store_y(e, pp):
                sp.wait_ge(y_done, e + 1 + ONE)
                settle(sp, sp_passed)
                sp.dma_start(y_s[bass.ds(e * CAP, CAP), :].rearrange("(i p) d -> p i d", p=P), yb[:, pp, :, :]).then_inc(y_out[pp], 16)

            sp.wait_ge(moe_const, 1)
            settle(sp, sp_passed)
            for k in range(NE * CAP // P // 2):
                sp.dma_start(slots_s[k * 2 * P:(k + 1) * 2 * P, :].rearrange("(p i) d -> p (i d)", i=2), zero[:, :]).then_inc(zeroed, 16)
            for pp in range(2):
                load_expert(pp, pp)
            for k in range(2):
                sp.wait_ge(post_out[k], 32 * NT // 2 + ONE)
                settle(sp, sp_passed)
            for k in range(4):
                sp.dma_start(hs[:, k, :], h2_s[k]).then_inc(hs_in[k], 16)
            with sp.Fori(1, NT // 4) as j:
                for k in range(4):
                    sp.wait_ge(scattered[k], 16 * j)
                    settle(sp, sp_passed)
                    sp.dma_start(hs[:, k, :], h2_s[4 * j + k]).then_inc(hs_in[k], 16)
            for k in range(4):
                sp.wait_ge(scattered[k], 16 * NT // 4)
                settle(sp, sp_passed)
            for pp in range(2):
                load_slots(pp, pp)
            with sp.Fori(1, NE // 2) as j:
                for pp in range(2):
                    e = 2 * j + pp
                    sp.wait_ge(y_mm, e - 1 + ONE)
                    settle(sp, sp_passed)
                    sp.wait_ge(y_done, e - 1 + ONE)
                    settle(sp, sp_passed)
                    load_expert(e, pp)
                    load_slots(e, pp)
                    store_y(e - 2, pp)
            for pp in range(2):
                store_y(NE - 2 + pp, pp)
            with sp.Fori(0, NT // 4) as j:
                for k in range(4):
                    t = 4 * j + k
                    sp.wait_ge(summed, 4 * j + ONE)
                    settle(sp, sp_passed)
                    sp.dma_start(fx[:, k, :], x1_s[t]).then_inc(fx_in[k], 16)
                for k in range(4):
                    sp.wait_ge(summed, 4 * j + k + 1 + ONE)
                    settle(sp, sp_passed)
                    sp.dma_start(out_d[4 * j + k], fo[:, k, :]).then_inc(out_done[k], 16)
            for k in range(4):
                sp.wait_ge(out_done[k], 16 * NT // 4 + ONE)
                settle(sp, sp_passed)

        @block.tensor
        def _(pe):
            start_counters(pe, [*scores_done, s["pv"], auxa_full, auxb_full, y_mm])
            pe.wait_ge(silu_done, 1)
            pe.wait_ge(mod_in, 48)
            banks = [XA, XB, Z]
            for k in range(3):
                for c, w in enumerate((wmod, wmod2)):
                    last = pe.matmul(banks[k][0:B, 0:HALF], sc[:, c * B:(c + 1) * B], w[:, k * HALF:(k + 1) * HALF],
                                     start=(c == 0), stop=(c == NC - 1))
            last.then_inc(mod_mm, 1)
            pe.wait_ge(mod_rows, 6)
            pe.wait_ge(consts, 5)
            pe.wait_ge(const_in, 80)

            def step(st):
                g, pp, ap = st.g, st.pp, st.att_par
                used = {"a": 0, "b": 0}

                def aux(which):
                    bank, free, name = (XA, auxa_free, "auxa") if which == "a" else (XB, auxb_free, "auxb")
                    pe.wait_ge(free, st.of(name, used[which]))
                    used[which] += 1
                    return bank

                def project(kind, half):
                    bank = aux("a" if half == 0 else "b")
                    if kind == "q" and half == 0:
                        pe.wait_ge(w_in[pp], 16 * (st.b * PAIRS // 2 + st.j + 1))
                        pe.wait_ge(auxb_free, st.n("auxb"))
                    if kind in "qk":
                        col = 0 if kind == "q" else P
                        for c in range(NC):
                            last = pe.matmul(bank[:, :], W[:, pp, c * QKV + col:c * QKV + col + P],
                                             hT[:, st.b % 2, c, half * HALF:(half + 1) * HALF],
                                             start=(c == 0), stop=(c == NC - 1))
                    else:
                        for t in range(4):
                            for c in range(NC):
                                tok = (4 * half + t) * P
                                last = pe.matmul(bank[:, t * P:(t + 1) * P], hT[:, st.b % 2, c, tok:tok + P],
                                                 W[:, pp, c * QKV + 2 * P:(c + 1) * QKV],
                                                 start=(c == 0), stop=(c == NC - 1))
                    last.then_inc(auxa_full if half == 0 else auxb_full, 1)
                    return last

                def score(kb, h):
                    pe.wait_ge(exp_done[h], st.of("expd", kb if kb <= 4 else kb - 1))
                    if kb == 0:
                        pe.wait_ge(qk_in[ap], qk_count(st))
                    lo = kb * P
                    spans = [(lo, HALF), (HALF, S)] if lo < HALF else [(lo, S)]
                    for a, z in spans:
                        at = a if kb < 4 else a - HALF + (kb % 2) * HALF
                        for part in range(2):
                            last = pe.matmul(SC[h][:, at:at + z - a], KS[:, ap, h, part, lo:lo + P],
                                             QS[:, ap, h, a:z], start=(part == 0), stop=(part == 1))
                    last.then_inc(scores_done[h], 1)

                def weigh(kb):
                    if kb == 0:
                        pe.wait_ge(s["zevac"], st.n("zevac"))
                    pe.wait_ge(s["vscaled"], st.of("vscaled", kb + 1))
                    lo = kb * P
                    spans = [(lo, HALF), (HALF, S)] if lo < HALF else [(lo, S)]
                    for a, z in spans:
                        for h in range(2):
                            last = pe.matmul(Z[DH * h:DH * h + DH, a:z], vs[:, kb % 2, DH * h:DH * h + DH],
                                             E[:, h, kb % 2, a:z], start=(kb == 0),
                                             stop=(kb == (3 if z == HALF else TPB - 1)))
                    last.then_inc(s["pv"], 1)

                for kb in range(TPB):
                    if st.has("att"):
                        score(kb, 0)
                        score(kb, 1)
                    if st.has("post") and kb == 0:
                        bank = aux("a")
                        pe.wait_ge(zx_in[pp], zx_count(st))
                        for c in range(PAIRS):
                            last = pe.matmul(bank[:, 0:D], zt[:, pp, c, :], woT[:, c, :], start=(c == 0), stop=(c == PAIRS - 1))
                        last.then_inc(auxa_full, 1)
                    if st.has("proj"):
                        for at, kind, half in ((1, "q", 0), (2, "q", 1), (3, "k", 0), (4, "k", 1), (5, "v", 0), (6, "v", 1)):
                            if kb == at:
                                last = project(kind, half)
                    if st.has("ln") and kb == 7:
                        bank = aux("b")
                        pe.wait_ge(s["hn"], st.of("hn", 1))
                        for c in range(NC):
                            last = pe.transpose(bank[:, c * P:(c + 1) * P], hn[:, c * P:(c + 1) * P], ident[:, :])
                        last.then_inc(auxb_full, 1)
                    if st.has("post") and kb == 6:
                        bank = aux("a")
                        pe.wait_ge(s["h2"], st.of("h2", 1))
                        for c in range(NC):
                            last = pe.transpose(bank[:, c * P:(c + 1) * P], h2[:, pp, c * P:(c + 1) * P], ident[:, :])
                        last.then_inc(auxa_full, 1)
                    if st.has("post") and kb == 7:
                        bank = aux("a")
                        for c in range(NC):
                            last = pe.matmul(bank[:, 0:NE], h2T[:, c, :], wg[:, c, :], start=(c == 0), stop=(c == NC - 1))
                        last.then_inc(auxa_full, 1)
                    if st.has("att") and kb >= 1:
                        weigh(kb - 1)
                if st.has("att"):
                    weigh(TPB - 1)

            run_steps(pe, step)

            pe.wait_ge(onehot, 1)
            pe.wait_ge(moe_const, 5)
            flat = oh[:, :, :].rearrange("p t e -> p (t e)")
            pe.matmul(XA[:, :], tri[:, :], flat, start=True, stop=True)
            pe.matmul(XB[:, :], ones[:, :], flat, start=True, stop=True).then_inc(prefix_mm, 1)
            pe.wait_ge(routed, 1)

            xbT = [XA, XB]
            hid = [SC[0][:, 0:HALF], SC[0][:, HALF:S], SC[1][:, 0:HALF], SC[1][:, HALF:S]]
            yps = [Z[:, 0:HALF], Z[:, HALF:S]]

            def expert(e, j, pp, more):
                pe.wait_ge(we_in[pp], 64 * (j + 1))
                pe.wait_ge(bT_done, e + 1)
                for m in range(4):
                    pe.wait_ge(hid_done[m], e + ONE)
                    for half in range(2):
                        for c in range(NC):
                            col = (2 * m + half) * P
                            last = pe.matmul(hid[m][:, half * CAP:(half + 1) * CAP], W1[:, pp, c, col:col + P],
                                             bT[:, pp, c, :], start=(c == 0), stop=(c == NC - 1))
                    last.then_inc(hid_mm[m], 1)
                if more:
                    transpose_rows_at(e + 1, j if pp == 0 else j + 1, 1 - pp)
                pe.wait_ge(y_done, e + ONE)
                for m in range(4):
                    pe.wait_ge(hid_done[m], e + 1 + ONE)
                for i in range(2):
                    for m in range(NM):
                        last = pe.matmul(yps[pp][:, i * D:(i + 1) * D], hh[:, m, i * P:(i + 1) * P], W2[:, pp, m, :],
                                         start=(m == 0), stop=(m == NM - 1))
                last.then_inc(y_mm, 1)

            def transpose_rows_at(e, j, pp):
                pe.wait_ge(bT_done, e)
                pe.wait_ge(xb_in[pp], 16 * (j + 1))
                for c in range(NC):
                    for i in range(2):
                        last = pe.transpose(xbT[pp][:, c * CAP + i * P:c * CAP + (i + 1) * P],
                                            xb[:, pp, i, c * P:(c + 1) * P], ident[:, :])
                last.then_inc(xbT_mm, 1)

            transpose_rows_at(0, 0, 0)
            with pe.Fori(0, NE // 2 - 1) as j:
                for pp in range(2):
                    expert(2 * j + pp, j, pp, True)
            expert(NE - 2, NE // 2 - 1, 0, True)
            expert(NE - 1, NE // 2 - 1, 1, False)

        @block.scalar
        def _(act):
            start_counters(act, [*exp_done, auxb_free, s["zevac"], s["hi"], s["ss"], hid_done[0], hid_done[2]])
            act.wait_ge(mod_in, 48)
            act.activation(ec[:, :], cT[:, :], ACT.Exp, scale=-1.0).then_inc(c_exp, 1)

            def step(st):
                pp, ap = st.pp, st.att_par
                for kb in range(TPB):
                    if st.has("att"):
                        lo = kb * P
                        at = lo if kb < 4 else lo - HALF + (kb % 2) * HALF
                        for h in range(2):
                            if h == 0:
                                act.wait_ge(s["pv"], st.of("pv", kb - 1 if kb else 0))
                            act.wait_ge(negmax_done[h], st.of("negmax", kb + 1))
                            act.activation(E[:, h, kb % 2, lo:S], SC[h][:, at:at + S - lo], ACT.Exp,
                                           bias=nm[:, h, kb:kb + 1], scale=-1.0,
                                           accum_out=rs[:, kb, h:h + 1]).then_inc(exp_done[h], 1)
                    if st.has("ln") and kb == 3:
                        act.wait_ge(s["h"], st.of("h", 1))
                        act.activation(hsq[:, :], hb[:, :], ACT.Square, accum_out=lss[:, :]).then_inc(s["ss"], 1)
                    if st.has("proj"):
                        for at_, n, bank in ((1, 0, XA), (2, 1, XB), (3, 2, XA), (4, 3, XB)):
                            if kb != at_:
                                continue
                            half = n % 2
                            full = auxa_full if half == 0 else auxb_full
                            name = "auxa" if half == 0 else "auxb"
                            first = 1 if half == 0 and st.has("post") else 0
                            act.wait_ge(full, st.of(name, first + n // 2 + 1))
                            if n == 0:
                                act.wait_ge(s["nbk"], st.of("nbk", 1))
                                act.wait_ge(qk_in[1 - pp], qk_count(st))
                            if n < 2:
                                act.activation(XQ[:, 0, half * HALF:(half + 1) * HALF], bank[:, :], ACT.Identity,
                                               bias=W[:, pp, WROW - 2:WROW - 1]).then_inc(s["hi"], 1)
                            else:
                                act.activation(XK[:, 0, half * HALF:(half + 1) * HALF], bank[:, :], ACT.Identity,
                                               bias=nbk[:, :], scale=-1.0).then_inc(s["hi"], 1)
                    if st.has("ln") and kb == 7:
                        act.wait_ge(auxb_full, st.of("auxb", 4 if st.has("proj") else 1))
                        act.activation(hT[:, (st.b + 1) % 2, :, bass.ds(st.i * P, P)],
                                       XB[:, 0:D].rearrange("p (c t) -> p c t", c=NC), ACT.Copy).then_inc(auxb_free, 1)
                    if st.has("post") and kb == 6:
                        act.wait_ge(auxa_full, st.of("auxa", 5 if st.has("proj") else 2))
                        act.activation(h2T[:, :, :], XA[:, 0:D].rearrange("p (c t) -> p c t", c=NC), ACT.Copy).then_inc(auxa_free, 1)
                if st.has("att"):
                    act.wait_ge(s["pv"], st.of("pv", TPB))
                    act.wait_ge(z_out, 16 * st.g)
                    act.activation(zs[:, :], Z[:, :], ACT.Copy).then_inc(s["zevac"], 1)

            run_steps(act, step)

            act.wait_ge(route_exp0, 1)
            act.activation(rb[:, :, :], ra[:, :, :], ACT.Exp).then_inc(route_exp, 1)
            hid = [SC[0][:, 0:HALF], SC[0][:, HALF:S], SC[1][:, 0:HALF], SC[1][:, HALF:S]]
            xbT = [XA, XB]

            def rows(e, pp):
                act.wait_ge(xbT_mm, e + 1)
                act.activation(bT[:, pp, :, :], xbT[pp][:, :].rearrange("p (c t) -> p c t", c=NC), ACT.Copy).then_inc(bT_done, 1)

            rows(0, 0)

            def expert(e, pp, more):
                act.wait_ge(y_mm, e + ONE)
                for m in (0, 2):
                    act.wait_ge(hid_mm[m], e + 1)
                    for half in range(2):
                        last = act.activation(hh[:, 2 * m + half, :], hid[m][:, half * CAP:(half + 1) * CAP], ACT.Relu,
                                              bias=b1t[:, pp, 2 * m + half:2 * m + half + 1])
                    last.then_inc(hid_done[m], 1)
                if more:
                    rows(e + 1, 1 - pp)

            with act.Fori(0, NE // 2 - 1) as j:
                for pp in range(2):
                    expert(2 * j + pp, pp, True)
            expert(NE - 2, 0, True)
            expert(NE - 1, 1, False)

        @block.vector
        def _(dve):
            start_counters(dve, [*negmax_done, auxa_free, hid_done[1], hid_done[3], y_done, scaled, summed])
            start_counters(dve, [s[n] for n in ("vscaled", "rowinv", "nbk", "xn", "lnve", "ms", "hn", "pve", "xn2", "dlink")])
            dve.wait_ge(c_exp, 1)
            dve.tensor_scalar(ec[:, :], ec[:, :], 1.0, None, ALU.add).then_inc(setup, 1)
            dve.wait_ge(setup, 1)
            dve.reciprocal(sc[:, :], ec[:, :]).then_inc(setup, 1)
            dve.wait_ge(setup, 2)
            dve.tensor_tensor(sc[:, :], sc[:, :], cT[:, :], ALU.mult).then_inc(silu_done, 1)
            dve.memset(mhalf[:, :], -0.5).then_inc(consts, 1)
            dve.wait_ge(mod_mm, 1)
            for k in range(6):
                src = [XA, XB, Z][k // 2][0:B, (k % 2) * D:(k % 2 + 1) * D]
                dst = modr[:, k * D:(k + 1) * D]
                if k in (SA, SB):
                    dve.tensor_copy(dst, src).then_inc(mod_rows, 1)
                elif k in (CA, CB):
                    dve.tensor_scalar(dst, src, 1.0, None, ALU.add).then_inc(mod_rows, 1)
                else:
                    n = 2 + 4 * (k == GB)
                    dve.wait_ge(mod_rows, k)
                    dve.tensor_scalar(sgn[:, 0, :], src, 0.0, 2.0, ALU.is_ge, ALU.mult).then_inc(setup, 1)
                    dve.wait_ge(setup, n + 1)
                    dve.tensor_scalar(sgn[:, 0, :], sgn[:, 0, :], -1.0, None, ALU.add).then_inc(setup, 1)
                    dve.tensor_scalar(sgn[:, 1, :], src, -1.0, 0.25, ALU.mult, ALU.max).then_inc(setup, 1)
                    dve.wait_ge(setup, n + 3)
                    dve.scalar_tensor_tensor(sgn[:, 1, :], src, 0.25, sgn[:, 1, :], ALU.max, ALU.max).then_inc(setup, 1)
                    dve.wait_ge(setup, n + 4)
                    dve.tensor_tensor(dst, sgn[:, 0, :], sgn[:, 1, :], ALU.mult).then_inc(mod_rows, 1)

            dve.wait_ge(consts, 5)
            dve.wait_ge(const_in, 80)

            def step(st):
                pp, ap = st.pp, st.att_par
                links = [0]

                def link(ins):
                    links[0] += 1
                    ins.then_inc(s["dlink"], 1)
                    dve.wait_ge(s["dlink"], st.of("dlink", links[0]))

                def stats(x, stt, mv, ve):
                    link(dve.bn_stats(stt[:, :], x))
                    settle(dve, dve_passed)
                    link(dve.bn_aggr(mv[:, :], stt[:, :]))
                    return dve.tensor_scalar(ve[:, :], mv[:, 1:2], LN_EPS, None, ALU.add)

                def scale_values(kb):
                    for h in range(2):
                        dve.wait_ge(exp_done[h], st.of("expd", kb + 1))
                    dve.reciprocal(ri[:, kb % 2, :], rs[:, kb, :]).then_inc(s["rowinv"], 1)
                    if kb >= 2:
                        dve.wait_ge(s["pv"], st.of("pv", kb - 1))
                    else:
                        dve.wait_ge(s["pv"], st.n("pv"))
                    dve.wait_ge(s["rowinv"], st.of("rowinv", kb + 1))
                    dve.tensor_tensor(vs[:, kb % 2, :].rearrange("p (h d) -> p h d", h=2),
                                      V[:, ap, kb, :].rearrange("p (h d) -> p h d", h=2),
                                      ri[:, kb % 2, :].unsqueeze(2).broadcast_to([P, 2, DH]), ALU.mult).then_inc(s["vscaled"], 1)

                for kb in range(TPB):
                    if st.has("att"):
                        lo = kb * P
                        at = lo if kb < 4 else lo - HALF + (kb % 2) * HALF
                        for h in range(2):
                            dve.wait_ge(scores_done[h], st.of("scores", kb + 1))
                            if kb == 0 and h == 0:
                                dve.wait_ge(auxa_free, st.n("auxa"))
                                dve.wait_ge(auxb_free, st.n("auxb"))
                            settle(dve, dve_passed)
                            dve.tensor_tensor_reduce(SC[h][:, at:at + S - lo], SC[h][:, at:at + S - lo], mask[:, 0:S - lo],
                                                     1.0, BIG, ALU.add, ALU.min, nm[:, h, kb:kb + 1]).then_inc(negmax_done[h], 1)
                    if st.has("proj") and kb == 0:
                        dve.wait_ge(w_in[pp], 16 * (st.b * PAIRS // 2 + st.j + 1))
                        dve.wait_ge(s["hi"], st.n("hi"))
                        dve.tensor_scalar(nbk[:, :], W[:, pp, WROW - 1:WROW], -1.0, None, ALU.mult).then_inc(s["nbk"], 1)
                        dve.wait_ge(s["nbk"], st.of("nbk", 1))
                    if st.has("ln"):
                        if kb == 0:
                            dve.wait_ge(xln_in[pp], 16 * ((st.b + 1) * PAIRS // 2 + st.j + 1))
                            stats(xln[:, pp, :], lst, lmv, lve).then_inc(s["lnve"], 1)
                        if kb == 1:
                            dve.wait_ge(s["rstd"], st.of("rstd", 1))
                            dve.wait_ge(s["h"], st.n("h"))
                            dve.tensor_scalar(xnb[:, :], xln[:, pp, :], lmv[:, 0:1], lrs[:, :], ALU.subtract,
                                              ALU.mult).then_inc(s["xn"], 1)
                        if kb == 4:
                            dve.wait_ge(s["ss"], st.of("ss", 1))
                            dve.tensor_scalar(lms[:, :], lss[:, :], 1.0 / D, RMS_EPS, ALU.mult, ALU.add).then_inc(s["ms"], 1)
                        if kb == 6:
                            dve.wait_ge(s["rr"], st.of("rr", 1))
                            dve.wait_ge(auxb_full, st.n("auxb"))
                            dve.tensor_scalar(hn[:, :], hb[:, :], lrr[:, :], None, ALU.mult).then_inc(s["hn"], 1)
                    if st.has("post"):
                        if kb == 1:
                            dve.wait_ge(auxa_full, st.of("auxa", 1))
                            dve.wait_ge(s["x1"], st.n("x1"))
                            dve.tensor_tensor(pt[:, :], XA[:, 0:D], boB[:, :], ALU.add).then_inc(auxa_free, 1)
                        if kb == 3:
                            dve.wait_ge(s["x1"], st.of("x1", 1))
                            stats(x1[:, pp, :], pst, pmv, pve).then_inc(s["pve"], 1)
                        if kb == 4:
                            dve.wait_ge(s["prstd"], st.of("prstd", 1))
                            dve.wait_ge(s["h2"], st.n("h2"))
                            dve.tensor_scalar(xn2[:, :], x1[:, pp, :], pmv[:, 0:1], prs[:, :], ALU.subtract,
                                              ALU.mult).then_inc(s["xn2"], 1)
                    if st.has("proj"):
                        for at_, n, bank in ((1, 0, XA), (2, 1, XB), (3, 2, XA), (4, 3, XB)):
                            if kb != at_:
                                continue
                            half = n % 2
                            cols = slice(half * HALF, (half + 1) * HALF)
                            dve.wait_ge(s["hi"], st.of("hi", n + 1))
                            free = auxa_free if half == 0 else auxb_free
                            if n < 2:
                                last = dve.scalar_tensor_tensor(XQ[:, 1, cols], bank[:, :], W[:, pp, WROW - 2:WROW - 1],
                                                                XQ[:, 0, cols].bitcast(F32), ALU.add, ALU.subtract)
                            else:
                                last = dve.scalar_tensor_tensor(XK[:, 1, cols], bank[:, :], nbk[:, :],
                                                                XK[:, 0, cols].bitcast(F32), ALU.subtract, ALU.subtract,
                                                                reverse0=True)
                            last.then_inc(free, 1)
                        for at_, half in ((5, 0), (6, 1)):
                            if kb != at_:
                                continue
                            full, name, free, bank = (auxa_full, "auxa", auxa_free, XA) if half == 0 else (auxb_full, "auxb", auxb_free, XB)
                            first = 1 if half == 0 and st.has("post") else 0
                            dve.wait_ge(full, st.of(name, first + 3))
                            col = st.i * P
                            last = dve.tensor_tensor(V[:, st.proj_par, 4 * half:4 * half + 4, :],
                                                     bank[:, :].rearrange("p (t d) -> p t d", t=4),
                                                     bvB[:, bass.ds(col, P)].unsqueeze(1).broadcast_to([P, 4, P]), ALU.add)
                            last.then_inc(free, 1)
                    if st.has("post") and kb == 7:
                        dve.wait_ge(auxa_full, st.of("auxa", 6 if st.has("proj") else 3))
                        dve.tensor_tensor(logits[:, bass.ds(st.tile, 1), :], XA[:, 0:NE].unsqueeze(1), bgB[:, :].unsqueeze(1), ALU.add)\
                            .then_inc(auxa_free, 1)
                    if st.has("att") and kb >= 1:
                        scale_values(kb - 1)
                if st.has("att"):
                    scale_values(TPB - 1)
                assert links[0] == sum(v for k, v in RISES["dlink"].items() if st.has(k))

            run_steps(dve, step)

            steps = [0]

            def link(ins):
                steps[0] += 1
                ins.then_inc(route, 1)
                dve.wait_ge(route, steps[0])

            def wide(a):
                return a.unsqueeze(2).broadcast_to([P, NT, NE])

            def each(a):
                return a.unsqueeze(1).broadcast_to([P, NT, NE])

            dve.wait_ge(auxa_free, TOTAL["auxa"])
            dve.wait_ge(moe_const, 5)
            link(dve.tensor_reduce(r1[:, :], logits[:, :, :], AX.X, ALU.max))
            dve.tensor_tensor(ra[:, :, :], logits[:, :, :], wide(r1[:, :]), ALU.subtract).then_inc(route_exp0, 1)
            dve.wait_ge(route_exp0, 1)
            link(dve.tensor_scalar(rc[:, :, :], ra[:, :, :], 0.0, None, ALU.is_ge))
            link(dve.tensor_tensor(rc[:, :, :], rc[:, :, :], each(revj[:, :]), ALU.mult))
            link(dve.tensor_reduce(r2[:, :], rc[:, :, :], AX.X, ALU.max))
            dve.tensor_tensor(oh[:, :, :], rc[:, :, :], wide(r2[:, :]), ALU.is_equal).then_inc(onehot, 1)
            dve.wait_ge(route_exp, 1)
            link(dve.tensor_reduce(r3[:, :], rb[:, :, :], AX.X, ALU.add))
            link(dve.reciprocal(r3[:, :], r3[:, :]))
            dve.wait_ge(onehot, 1)
            link(dve.tensor_tensor(rc[:, :, :], oh[:, :, :], each(ebase[:, :]), ALU.mult))
            link(dve.tensor_reduce(r4[:, :], rc[:, :, :], AX.X, ALU.add))
            dve.wait_ge(prefix_mm, 1)
            link(dve.memset(base[:, 0, :], 0.0))
            tot = XB[:, :].rearrange("p (t e) -> p t e", t=NT)
            for t in range(1, NT):
                link(dve.tensor_tensor(base[:, t, :], base[:, t - 1, :], tot[:, t - 1, :], ALU.add))
            link(dve.tensor_tensor(ra[:, :, :], XA[:, :].rearrange("p (t e) -> p t e", t=NT), base[:, :, :], ALU.add))
            link(dve.tensor_tensor(ra[:, :, :], ra[:, :, :], oh[:, :, :], ALU.mult))
            link(dve.tensor_reduce(r1[:, :], ra[:, :, :], AX.X, ALU.add))
            link(dve.tensor_scalar(keepm[:, :], r1[:, :], float(CAP), None, ALU.is_lt))
            link(dve.tensor_tensor(gates[:, :], r3[:, :], keepm[:, :], ALU.mult))
            link(dve.tensor_tensor(r1[:, :], r1[:, :], r4[:, :], ALU.add))
            link(dve.tensor_scalar(r2[:, :], keepm[:, :], -FAR, FAR, ALU.mult, ALU.add))
            dve.tensor_tensor(slot_u[:, :], r1[:, :], r2[:, :], ALU.add).then_inc(routed, 1)

            hid = [SC[0][:, 0:HALF], SC[0][:, HALF:S], SC[1][:, 0:HALF], SC[1][:, HALF:S]]

            def expert(e, j, pp):
                dve.wait_ge(y_mm, e + ONE)
                for m in (1, 3):
                    dve.wait_ge(hid_mm[m], e + 1)
                    for half in range(2):
                        last = dve.tensor_scalar(hh[:, 2 * m + half, :], hid[m][:, half * CAP:(half + 1) * CAP],
                                                 b1t[:, pp, 2 * m + half:2 * m + half + 1], 0.0, ALU.add, ALU.max)
                    last.then_inc(hid_done[m], 1)
                dve.wait_ge(y_mm, e + 1 + ONE)
                dve.wait_ge(y_out[pp], 16 * j + ONE)
                dve.tensor_tensor(yb[:, pp, :, :], Z[:, pp * HALF:(pp + 1) * HALF].rearrange("p (i d) -> p i d", i=2),
                                  b2B[:, pp, :].unsqueeze(1).broadcast_to([P, 2, D]), ALU.add).then_inc(y_done, 1)

            with dve.Fori(0, NE // 2) as j:
                for pp in range(2):
                    expert(2 * j + pp, j, pp)

            with dve.Fori(0, NT // 4) as j:
                for k in range(4):
                    t = 4 * j + k
                    dve.wait_ge(gat_in[k], 16 * (j + 1))
                    dve.wait_ge(summed, 4 * j + max(0, k - 1) + ONE)
                    dve.scalar_tensor_tensor(ft[:, k % 2, :], gat[:, k, :], gcol[:, k:k + 1], modB[:, t // TPB, GB, :],
                                             ALU.mult, ALU.mult).then_inc(scaled, 1)
                    dve.wait_ge(scaled, t + 1 + ONE)
                    dve.wait_ge(fx_in[k], 16 * (j + 1))
                    dve.wait_ge(out_done[k], 16 * j + ONE)
                    dve.tensor_tensor(fo[:, k, :], ft[:, k % 2, :], fx[:, k, :], ALU.add).then_inc(summed, 1)

        @block.gpsimd
        def _(pool):
            start_counters(pool, [s[n] for n in ("rstd", "h", "rr", "x1", "prstd", "h2", "plink")])
            pool.memset(ident[:, :], 0.0).then_inc(consts, 1)
            pool.memset(mask[:, :], 0.0).then_inc(consts, 1)
            pool.wait_ge(consts, 3)
            pool.affine_select(ident[:, :], ident[:, :], pattern=[[-1, P]], compare_op=ALU.not_equal, fill=1.0,
                               base=0, channel_multiplier=1).then_inc(consts, 1)
            pool.affine_select(mask[:, 0:P], mask[:, 0:P], pattern=[[1, P]], compare_op=ALU.is_ge, fill=BIG,
                               base=0, channel_multiplier=-1).then_inc(consts, 1)
            pool.wait_ge(modb_in, 16)

            def step(st):
                pp = st.pp
                links = [0]

                def link(ins):
                    links[0] += 1
                    ins.then_inc(s["plink"], 1)
                    pool.wait_ge(s["plink"], st.of("plink", links[0]))

                if st.has("ln"):
                    pool.wait_ge(s["lnve"], st.of("lnve", 1))
                    pool.tensor_tensor(lrs[:, :], lve[:, :], mhalf[:, :], ALU.pow).then_inc(s["rstd"], 1)
                    pool.wait_ge(s["xn"], st.of("xn", 1))
                    link(pool.tensor_tensor(ha[:, :], xnb[:, :], modB[:, st.b + 1, CA, :], ALU.mult))
                    pool.wait_ge(s["hn"], st.n("hn"))
                    pool.tensor_tensor(hb[:, :], ha[:, :], modB[:, st.b + 1, SA, :], ALU.add).then_inc(s["h"], 1)
                if st.has("post"):
                    bt = st.tile // TPB
                    pool.wait_ge(auxa_free, st.of("auxa", 1))
                    link(pool.tensor_tensor(pt2[:, :].unsqueeze(1), pt[:, :].unsqueeze(1), modB[:, bass.ds(bt, 1), GA, :], ALU.mult))
                    pool.wait_ge(zx_in[pp], zx_count(st))
                    pool.wait_ge(post_out[pp], zx_count(st) - 32 + ONE)
                    pool.tensor_tensor(x1[:, pp, :], pt2[:, :], xp[:, pp, :], ALU.add).then_inc(s["x1"], 1)
                if st.has("ln"):
                    pool.wait_ge(s["ms"], st.of("ms", 1))
                    pool.tensor_tensor(lrr[:, :], lms[:, :], mhalf[:, :], ALU.pow).then_inc(s["rr"], 1)
                if st.has("post"):
                    pool.wait_ge(s["pve"], st.of("pve", 1))
                    pool.tensor_tensor(prs[:, :], pve[:, :], mhalf[:, :], ALU.pow).then_inc(s["prstd"], 1)
                    pool.wait_ge(s["xn2"], st.of("xn2", 1))
                    link(pool.tensor_tensor(h2a[:, :].unsqueeze(1), xn2[:, :].unsqueeze(1), modB[:, bass.ds(bt, 1), CB, :], ALU.mult))
                    pool.tensor_tensor(h2[:, pp, :].unsqueeze(1), h2a[:, :].unsqueeze(1), modB[:, bass.ds(bt, 1), SB, :], ALU.add).then_inc(s["h2"], 1)

            run_steps(pool, step)

            pool.wait_ge(s["zevac"], TOTAL["zevac"])
            pool.wait_ge(z_out, 16 * NG)
            pool.memset(zero[:, :], 0.0).then_inc(moe_const, 1)
            pool.memset(ones[:, :], 1.0).then_inc(moe_const, 1)
            pool.wait_ge(moe_const, 2)
            pool.affine_select(tri[:, :], ones[:, :], pattern=[[1, P]], compare_op=ALU.is_gt, fill=0.0,
                               base=0, channel_multiplier=-1).then_inc(moe_const, 1)
            pool.iota(revj[:, :], pattern=[[-1, NE]], base=NE, channel_multiplier=0,
                      allow_small_or_imprecise_dtypes=True).then_inc(moe_const, 1)
            pool.iota(ebase[:, :], pattern=[[CAP, NE]], base=0, channel_multiplier=0,
                      allow_small_or_imprecise_dtypes=True).then_inc(moe_const, 1)
            pool.wait_ge(routed, 1)
            pool.wait_ge(zeroed, 16 * (NE * CAP // P // 2))

            def scatter(j):
                for k in range(4):
                    if not isinstance(j, int):
                        pool.wait_ge(scattered[k], 16 * j)
                    pool.tensor_copy(idx[:, k:k + 1], slot_u[:, bass.ds(4 * j + k, 1)]).then_inc(idx_ok, 1)
                    pool.wait_ge(idx_ok, 4 * j + k + 1)
                    pool.wait_ge(hs_in[k], 16 * (j + 1))
                    settle(pool, pool_passed)
                    pool.indirect_dma_start(slots_s, bass.IndirectOffsetOnAxis(idx[:, k:k + 1], 0), hs[:, k, :], None,
                                            bounds_check=NE * CAP - 1, oob_is_err=False).then_inc(scattered[k], 16)

            scatter(0)
            with pool.Fori(1, NT // 4) as j:
                scatter(j)
            for k in range(4):
                pool.wait_ge(scattered[k], 16 * (NT // 4))
            for pp in range(2):
                pool.wait_ge(y_out[pp], 16 * NE // 2 + ONE)
            with pool.Fori(0, NT // 4) as j:
                for k in range(4):
                    pool.wait_ge(scaled, 4 * j + ONE)
                    pool.tensor_copy(idx[:, k:k + 1], slot_u[:, bass.ds(4 * j + k, 1)]).then_inc(idx_ok, 1)
                    pool.tensor_copy(gcol[:, k:k + 1], gates[:, bass.ds(4 * j + k, 1)]).then_inc(gat_clear, 1)
                    pool.memset(gat[:, k, :], 0.0).then_inc(gat_clear, 1)
                    pool.wait_ge(idx_ok, NT + 4 * j + k + 1)
                    pool.wait_ge(gat_clear, 8 * j + 2 * k + 2)
                    settle(pool, pool_passed)
                    pool.indirect_dma_start(gat[:, k, :], None, y_s, bass.IndirectOffsetOnAxis(idx[:, k:k + 1], 0),
                                            bounds_check=NE * CAP - 1, oob_is_err=False).then_inc(gat_in[k], 16)


def kernel(**inputs):
    import numpy as np
    import concourse.bacc as bacc
    from concourse.bass_utils import run_bass_kernel_spmd

    a = {k: np.asarray(v) for k, v in inputs.items()}
    w = a["L0_attn_W_qkv"].reshape(PAIRS, 2, DH, 3, NC, P).transpose(0, 5, 4, 3, 1, 2).reshape(PAIRS, P, NC * QKV)
    bqkv = a["L0_attn_b_qkv"].reshape(PAIRS, P, 3)
    arrays = {
        "x": a["L0_attn_x"].reshape(NT, P, D),
        "wqkv": np.concatenate([w, bqkv[:, :, 0:2]], axis=2),
        "bv": bqkv[:, :, 2].reshape(1, PAIRS * P),
        "wo": a["L0_attn_W_o"].T.reshape(PAIRS, P, D).transpose(1, 0, 2),
        "bo": a["L0_attn_b_o"].reshape(1, D),
        "wg": a["L0_ffn_Wg"].reshape(NC, P, NE).transpose(1, 0, 2),
        "bg": a["L0_ffn_bg"].reshape(1, NE),
        "w1": a["L0_ffn_W1"],
        "b1": a["L0_ffn_b1"].reshape(NE, NM, P).transpose(0, 2, 1),
        "w2": a["L0_ffn_W2"],
        "b2": a["L0_ffn_b2"],
        "c": a["L0_c"].reshape(B, NC, P).transpose(2, 1, 0).reshape(P, NC * B),
        "wmod": a["L0_wmod"].reshape(NC, P, 6 * D),
    }
    nc = bacc.Bacc("TRN2", target_bir_lowering=False, num_devices=1)
    feeds, args = {}, []
    for name, v in arrays.items():
        v = np.ascontiguousarray(v)
        feeds[f"in_{name}"] = v
        args.append(nc.dram_tensor(f"in_{name}", v.shape, mybir.dt.from_np(v.dtype), kind="ExternalInput").ap())
    args.append(nc.dram_tensor("out", [NT, P, D], F32, kind="ExternalOutput").ap())
    adaln_block(nc, *args)
    r = run_bass_kernel_spmd(nc, [feeds], core_ids=[0])
    return r.results[0]["out"].reshape(B, S, D)
```

```python
from contextlib import ExitStack

import concourse.bass as bass
from concourse import mybir

P = 128
B, S, D = 4, 1024, 256
H, DH = 16, 64
PAIRS = H // 2
NG = B * PAIRS
TPB = S // P
NT = B * TPB
NC = D // P
NE, HID = 16, 1024
NM = HID // P
CAP = B * S // NE
HALF = 512
LAG = PAIRS + 1
QKV = 3 * P
WROW = NC * QKV + 2
LN_EPS = 1e-5
RMS_EPS = 1.1920929e-07
BIG = 3.0e38
FAR = float(1 << 20)

ALU = mybir.AluOpType
ACT = mybir.ActivationFunctionType
AX = mybir.AxisListType
F32 = mybir.dt.float32
F32R = mybir.dt.float32r
U32 = mybir.dt.uint32

ONE = 1

SA, CA, GA, SB, CB, GB = range(6)

RISES = {
    "scores": dict(att=TPB), "negmax": dict(att=TPB), "expd": dict(att=TPB), "vscaled": dict(att=TPB),
    "rowinv": dict(att=TPB), "pv": dict(att=TPB), "zevac": dict(att=1),
    "auxa": dict(post=1, proj=3, ln=1), "auxb": dict(proj=3, post=2),
    "hi": dict(proj=4), "wsplit": dict(proj=1), "hThi": dict(ln=1),
    "xn": dict(ln=1), "lnve": dict(ln=1), "rstd": dict(ln=1), "h": dict(ln=1), "ss": dict(ln=1), "ms": dict(ln=1),
    "rr": dict(ln=1), "hn": dict(ln=1),
    "x1": dict(post=1), "pve": dict(post=1), "prstd": dict(post=1), "xn2": dict(post=1),
    "h2": dict(post=1),
    "dlink": dict(ln=2, post=2), "plink": dict(ln=1, post=2, proj=1),
}


class Step:

    def __init__(self, seg, b, j, pp, before, since):
        self.seg, self.b, self.j, self.pp, self.before, self.since = seg, b, j, pp, before, since
        self.i = 2 * j + pp
        self.g = b * PAIRS - 1 + self.i
        self.tile = self.g - LAG
        self.att_par, self.proj_par = 1 - pp, pp

    def has(self, part):
        return part in self.seg

    def n(self, name):
        per = sum(v for k, v in RISES[name].items() if k in self.seg)
        return self.before[name] + per * self.since

    def of(self, name, k):
        return self.n(name) + k


PROJECTIONS = {0: ("q", 0), 1: ("q", 1), 2: ("k", 0), 3: ("k", 1), 4: ("v", 0), 6: ("v", 1)}

SEGS = [
    (-1, 0, 4, (0, 1), ("ln",)),
    (0, 0, 1, (0,), ("proj", "ln")),
    (0, 0, 1, (1,), ("att", "proj", "ln")),
    (0, 1, 4, (0, 1), ("att", "proj", "ln")),
    (1, 0, 1, (0, 1), ("att", "proj", "ln")),
    (1, 1, 4, (0, 1), ("att", "proj", "ln", "post")),
    (2, 0, 4, (0, 1), ("att", "proj", "ln", "post")),
    (3, 0, 4, (0, 1), ("att", "proj", "post")),
    (4, 0, 1, (0,), ("att", "post")),
    (4, 0, 1, (1,), ("post",)),
    (4, 1, 5, (0, 1), ("post",)),
]


def rises_before(k):
    done = {name: ONE for name in RISES}
    for b, j0, j1, halves, parts in SEGS[:k]:
        steps = (j1 - j0) * len(halves)
        for name, per in RISES.items():
            done[name] += steps * sum(v for part, v in per.items() if part in parts)
    return done


def run_steps(eng, body):
    for k, (b, j0, j1, halves, parts) in enumerate(SEGS):
        before = rises_before(k)
        if j1 - j0 == 1:
            for n, pp in enumerate(halves):
                body(Step(parts, b, j0, pp, before, n))
        else:
            with eng.Fori(j0, j1) as j:
                for pp in halves:
                    body(Step(parts, b, j, pp, before, 2 * (j - j0) + pp))


TOTAL = rises_before(len(SEGS))


def start_counters(eng, sems):
    for x in sems:
        eng.sem_inc(x, ONE)


def settle(eng, passed):
    eng.sem_inc(passed, 1)


def qk_count(st):
    return 8 * 16 * (st.b * PAIRS // 2 + st.j + st.pp)


def zx_count(st):
    return 32 * (st.b * PAIRS // 2 + st.j - (LAG + 1) // 2 + 1)


def adaln_block(nc, x_d, wqkv_d, bv_d, wo_d, bo_d, wg_d, bg_d, w1_d, b1_d, w2_d, b2_d, c_d, wmod_d, out_d):
    keep = ExitStack()
    with keep:
        def dram(name, shape, dt=F32):
            return nc.dram_tensor(name, shape, dt, kind="Internal").ap()

        def sb(name, shape, dt=F32, stack=keep):
            return stack.enter_context(nc.sbuf_tensor(name, shape, dt))

        def sem(name):
            return keep.enter_context(nc.semaphore(name))

        mod_s = dram("mod_s", [B, 6 * D])
        z_s = dram("z_s", [NG, P, S])
        x1_s = dram("x1_s", [NT, P, D])
        h2_s = dram("h2_s", [NT, P, D])
        slots_s = dram("slots_s", [NE * CAP, D])
        y_s = dram("y_s", [NE * CAP, D])

        ident = sb("ident", [P, P])
        modB = sb("modB", [P, B, 6, D])
        logits = sb("logits", [P, NT, NE])
        slot_u = sb("slot_u", [P, NT], U32)
        gates = sb("gates", [P, NT])
        mhalf = sb("mhalf", [P, 1])

        woT = sb("woT", [P, PAIRS, D])
        boB = sb("boB", [P, D])
        wg = sb("wg", [P, NC, NE])
        bgB = sb("bgB", [P, NE])
        zt = sb("zt", [P, 2, PAIRS, P])
        xp = sb("xp", [P, 2, D])
        pt = sb("pt", [P, D])
        x1 = sb("x1", [P, 2, D])
        xn2 = sb("xn2", [P, D])
        h2 = sb("h2", [P, 2, D])
        h2T = sb("h2T", [P, NC, P])
        pst = sb("pst", [P, 6])
        pmv = sb("pmv", [P, 2])
        pve = sb("pve", [P, 1])
        prs = sb("prs", [P, 1])

        att = ExitStack()
        E = sb("E", [P, 2, 2, S], stack=att)
        QS = sb("QS", [P, 2, 2, S], F32R, stack=att)
        KS = sb("KS", [P, 2, 2, 2, S], F32R, stack=att)
        XQ = sb("XQ", [P, 2, S], F32R, stack=att)
        XK = sb("XK", [P, 2, S], F32R, stack=att)
        V = sb("V", [P, 2, TPB, P], stack=att)
        vs = sb("vs", [P, 2, P], stack=att)
        rs = sb("rs", [P, TPB, 2], stack=att)
        ri = sb("ri", [P, 2, 2], stack=att)
        nm = sb("nm", [P, 2, TPB], stack=att)
        mask = sb("mask", [P, S], stack=att)
        hTh = sb("hTh", [P, 2, NC, S], F32R, stack=att)
        hTl = sb("hTl", [P, 2, NC, S], F32R, stack=att)
        W = sb("W", [P, WROW], stack=att)
        Wh = sb("Wh", [P, 2, NC * QKV], F32R, stack=att)
        Wl = sb("Wl", [P, 2, NC * QKV], F32R, stack=att)
        qkb = sb("qkb", [P, 2, 2], stack=att)
        bvB = sb("bvB", [P, PAIRS * P], stack=att)
        zs = sb("zs", [P, S], stack=att)
        xln = sb("xln", [P, 2, D], stack=att)
        xnb = sb("xnb", [P, D], stack=att)
        ha = sb("ha", [P, D], stack=att)
        hsq = sb("hsq", [P, D], stack=att)
        hn = sb("hn", [P, D], stack=att)
        lst = sb("lst", [P, 6], stack=att)
        lmv = sb("lmv", [P, 2], stack=att)
        lve = sb("lve", [P, 1], stack=att)
        lrs = sb("lrs", [P, 1], stack=att)
        lss = sb("lss", [P, 1], stack=att)
        lms = sb("lms", [P, 1], stack=att)
        lrr = sb("lrr", [P, 1], stack=att)
        wmod = E[:, 0, :, :].rearrange("p a b -> p (a b)")
        wmod2 = E[:, 1, :, :].rearrange("p a b -> p (a b)")
        cT = sb("cT", [P, NC * B], stack=att)
        ec = sb("ec", [P, NC * B], stack=att)
        sc = sb("sc", [P, NC * B], stack=att)
        modr = V[0:B, :, :, :].rearrange("p a b c -> p (a b c)")[:, 0:6 * D]
        sgn = zs[0:B, 0:2 * D].rearrange("p (a d) -> p a d", a=2)
        att.close()

        moe = ExitStack()
        keep.enter_context(moe)
        W1 = sb("W1", [P, 2, NC, HID])
        W2 = sb("W2", [P, 2, NM, D])
        b1t = sb("b1t", [P, 2, NM])
        b2B = sb("b2B", [P, 2, D])
        zero = sb("zero", [P, 2 * D])
        tri = sb("tri", [P, P])
        ones = sb("ones", [P, P])
        revj = sb("revj", [P, NE])
        ebase = sb("ebase", [P, NE])
        ra = sb("ra", [P, NT, NE])
        rb = sb("rb", [P, NT, NE])
        rc = sb("rc", [P, NT, NE])
        oh = sb("oh", [P, NT, NE])
        base = sb("base", [P, NT, NE])
        r1 = sb("r1", [P, NT])
        r2 = sb("r2", [P, NT])
        r3 = sb("r3", [P, NT])
        r4 = sb("r4", [P, NT])
        keepm = sb("keepm", [P, NT])
        hs = sb("hs", [P, 4, D])
        idx = sb("idx", [P, 4], U32)
        gcol = sb("gcol", [P, 4])
        xb = sb("xb", [P, 2, 2, D])
        bT = sb("bT", [P, 2, NC, CAP])
        hh = sb("hh", [P, NM, CAP])
        yb = sb("yb", [P, 2, 2, D])
        gat = sb("gat", [P, 4, D])
        fx = sb("fx", [P, 4, D])
        ft = sb("ft", [P, 2, D])
        fo = sb("fo", [P, 4, D])

        SC = [keep.enter_context(nc.psum_tensor(f"SC{h}", [P, S], F32)) for h in range(2)]
        Z = keep.enter_context(nc.psum_tensor("Z", [P, S], F32))
        XA = keep.enter_context(nc.psum_tensor("XA", [P, HALF], F32))
        XB = keep.enter_context(nc.psum_tensor("XB", [P, HALF], F32))

        names = [n for n in RISES if n not in ("scores", "negmax", "expd")]
        s = {n: sem("s_" + n) for n in names}
        scores_done = [sem(f"scores_done{h}") for h in range(2)]
        negmax_done = [sem(f"negmax_done{h}") for h in range(2)]
        exp_done = [sem(f"exp_done{h}") for h in range(2)]
        auxa_full, auxa_free = s["auxa"], sem("auxa_free")
        auxb_full, auxb_free = s["auxb"], sem("auxb_free")
        w_in = sem("w_in")
        qk_in = [sem(f"qk_in{k}") for k in range(2)]
        xln_in = [sem(f"xln_in{k}") for k in range(2)]
        zx_in = [sem(f"zx_in{k}") for k in range(2)]
        z_out = sem("z_out")
        post_out = [sem(f"post_out{k}") for k in range(2)]
        const_in = sem("const_in")
        mod_in = sem("mod_in")
        mod_out = sem("mod_out")
        modb_in = sem("modb_in")
        consts = sem("consts")
        c_exp = sem("c_exp")
        setup = sem("setup")
        silu_done = sem("silu_done")
        mod_mm = sem("mod_mm")
        mod_rows = sem("mod_rows")
        setup_split = sem("setup_split")

        zeroed = sem("zeroed")
        moe_const = sem("moe_const")
        route = sem("route")
        route_exp0 = sem("route_exp0")
        route_exp = sem("route_exp")
        onehot = sem("onehot")
        prefix_mm = sem("prefix_mm")
        routed = sem("routed")
        hs_in = [sem(f"hs_in{k}") for k in range(4)]
        idx_ok = sem("idx_ok")
        scattered = [sem(f"scattered{k}") for k in range(4)]
        we_in = [sem(f"we_in{k}") for k in range(2)]
        xb_in = [sem(f"xb_in{k}") for k in range(2)]
        xbT_mm = sem("xbT_mm")
        bT_done = sem("bT_done")
        hid_mm = [sem(f"hid_mm{m}") for m in range(4)]
        hid_done = [sem(f"hid_done{m}") for m in range(4)]
        y_mm = sem("y_mm")
        y_done = sem("y_done")
        y_out = [sem(f"y_out{k}") for k in range(2)]
        gat_clear = sem("gat_clear")
        gat_in = [sem(f"gat_in{k}") for k in range(4)]
        fx_in = [sem(f"fx_in{k}") for k in range(4)]
        scaled = sem("scaled")
        summed = sem("summed")
        out_done = [sem(f"out_done{k}") for k in range(4)]

        sp_passed, dve_passed, pool_passed = sem("sp_passed"), sem("dve_passed"), sem("pool_passed")

        block = keep.enter_context(nc.Block())

        @block.sync
        def _(sp):
            start_counters(sp, [*post_out, *y_out, *out_done])
            sp.dma_start(cT[:, :], c_d).then_inc(mod_in, 16)
            sp.dma_start(wmod[:, 0:6 * D], wmod_d[0]).then_inc(mod_in, 16)
            sp.dma_start(wmod2[:, 0:6 * D], wmod_d[1]).then_inc(mod_in, 16)
            sp.dma_start(W[:, :], wqkv_d[0]).then_inc(w_in, 16)
            sp.dma_start(woT[:, :, :], wo_d).then_inc(const_in, 16)
            sp.dma_start(boB[:, :], bo_d.broadcast_to([P, D])).then_inc(const_in, 16)
            sp.dma_start(wg[:, :, :], wg_d).then_inc(const_in, 16)
            sp.dma_start(bgB[:, :], bg_d.broadcast_to([P, NE])).then_inc(const_in, 16)
            sp.dma_start(bvB[:, :], bv_d.broadcast_to([P, PAIRS * P])).then_inc(const_in, 16)
            sp.wait_ge(mod_rows, 6)
            sp.dma_start(mod_s, modr).then_inc(mod_out, 16)
            sp.wait_ge(mod_out, 16)
            sp.dma_start(modB[:, :, :, :].rearrange("p b k d -> p (b k d)"),
                         mod_s.rearrange("b n -> (b n)").unsqueeze(0).broadcast_to([P, B * 6 * D])).then_inc(modb_in, 16)

            def step(st):
                g = st.g
                if st.has("post"):
                    t = st.tile
                    bt = t // TPB
                    tt = t % TPB
                    sp.wait_ge(z_out, 16 * (g - 1 if st.has("att") else NG))
                    settle(sp, sp_passed)
                    sp.wait_ge(s["x1"], st.n("x1"))
                    settle(sp, sp_passed)
                    sp.dma_start(zt[:, st.pp, :, :],
                                 z_s[bass.ds(bt * PAIRS, PAIRS), :, bass.ds(tt * P, P)].rearrange("c p t -> p c t")).then_inc(zx_in[st.pp], 16)
                    sp.dma_start(xp[:, st.pp, :], x_d[t]).then_inc(zx_in[st.pp], 16)
                if st.has("proj"):
                    sp.wait_ge(s["wsplit"], st.of("wsplit", 1))
                    settle(sp, sp_passed)
                    sp.dma_start(W[:, :], wqkv_d[(st.i + 1) % PAIRS]).then_inc(w_in, 16)
                if st.has("ln"):
                    sp.wait_ge(s["xn"], st.n("xn"))
                    settle(sp, sp_passed)
                    sp.dma_start(xln[:, st.pp, :], x_d[(st.b + 1) * TPB + st.i]).then_inc(xln_in[st.pp], 16)
                if st.has("proj"):
                    sp.wait_ge(s["hi"], st.of("hi", 4))
                    settle(sp, sp_passed)
                    sp.wait_ge(auxa_free, st.of("auxa", st.has("post") + 2))
                    settle(sp, sp_passed)
                    sp.wait_ge(auxb_free, st.of("auxb", 2))
                    settle(sp, sp_passed)
                    sp.wait_ge(scores_done[1], st.n("scores"))
                    settle(sp, sp_passed)
                    for h in range(2):
                        rows = slice(DH * h, DH * h + DH)
                        for part in range(2):
                            to = slice(DH * part, DH * part + DH)
                            sp.dma_start(QS[to, st.proj_par, h, :].bitcast(F32), XQ[rows, part, :].bitcast(F32)).then_inc(qk_in[st.proj_par], 16)
                            sp.dma_start(KS[to, st.proj_par, h, :, :].bitcast(F32), XK[rows, :, :].bitcast(F32)).then_inc(qk_in[st.proj_par], 16)
                if st.has("post"):
                    sp.wait_ge(s["x1"], st.of("x1", 1))
                    settle(sp, sp_passed)
                    sp.dma_start(x1_s[t], x1[:, st.pp, :]).then_inc(post_out[st.pp], 16)
                    sp.wait_ge(s["h2"], st.of("h2", 1))
                    settle(sp, sp_passed)
                    sp.dma_start(h2_s[t], h2[:, st.pp, :]).then_inc(post_out[st.pp], 16)

            run_steps(sp, step)

            sp.wait_ge(s["pv"], TOTAL["pv"])
            settle(sp, sp_passed)
            sp.wait_ge(s["zevac"], TOTAL["zevac"])
            settle(sp, sp_passed)
            sp.wait_ge(z_out, 16 * NG)
            settle(sp, sp_passed)

            def load_expert(e, pp):
                sp.dma_start(W1[:, pp, :, :], w1_d[e].rearrange("(c p) n -> p c n", p=P)).then_inc(we_in[pp], 16)
                sp.dma_start(W2[:, pp, :, :], w2_d[e].rearrange("(m p) n -> p m n", p=P)).then_inc(we_in[pp], 16)
                sp.dma_start(b1t[:, pp, :], b1_d[e]).then_inc(we_in[pp], 16)
                sp.dma_start(b2B[:, pp, :], b2_d[e].unsqueeze(0).broadcast_to([P, D])).then_inc(we_in[pp], 16)

            def load_slots(e, pp):
                sp.dma_start(xb[:, pp, :, :], slots_s[bass.ds(e * CAP, CAP), :].rearrange("(i p) d -> p i d", p=P)).then_inc(xb_in[pp], 16)

            def store_y(e, pp):
                sp.wait_ge(y_done, e + 1 + ONE)
                settle(sp, sp_passed)
                sp.dma_start(y_s[bass.ds(e * CAP, CAP), :].rearrange("(i p) d -> p i d", p=P), yb[:, pp, :, :]).then_inc(y_out[pp], 16)

            sp.wait_ge(moe_const, 1)
            settle(sp, sp_passed)
            for k in range(NE * CAP // P // 2):
                sp.dma_start(slots_s[k * 2 * P:(k + 1) * 2 * P, :].rearrange("(p i) d -> p (i d)", i=2), zero[:, :]).then_inc(zeroed, 16)
            for pp in range(2):
                load_expert(pp, pp)
            for k in range(2):
                sp.wait_ge(post_out[k], 32 * NT // 2 + ONE)
                settle(sp, sp_passed)
            for k in range(4):
                sp.dma_start(hs[:, k, :], h2_s[k]).then_inc(hs_in[k], 16)
            with sp.Fori(1, NT // 4) as j:
                for k in range(4):
                    sp.wait_ge(scattered[k], 16 * j)
                    settle(sp, sp_passed)
                    sp.dma_start(hs[:, k, :], h2_s[4 * j + k]).then_inc(hs_in[k], 16)
            for k in range(4):
                sp.wait_ge(scattered[k], 16 * NT // 4)
                settle(sp, sp_passed)
            for pp in range(2):
                load_slots(pp, pp)
            with sp.Fori(1, NE // 2) as j:
                for pp in range(2):
                    e = 2 * j + pp
                    sp.wait_ge(y_mm, e - 1 + ONE)
                    settle(sp, sp_passed)
                    sp.wait_ge(y_done, e - 1 + ONE)
                    settle(sp, sp_passed)
                    load_expert(e, pp)
                    load_slots(e, pp)
                    store_y(e - 2, pp)
            for pp in range(2):
                store_y(NE - 2 + pp, pp)
            with sp.Fori(0, NT // 4) as j:
                for k in range(4):
                    t = 4 * j + k
                    sp.wait_ge(summed, 4 * j + ONE)
                    settle(sp, sp_passed)
                    sp.dma_start(fx[:, k, :], x1_s[t]).then_inc(fx_in[k], 16)
                for k in range(4):
                    sp.wait_ge(summed, 4 * j + k + 1 + ONE)
                    settle(sp, sp_passed)
                    sp.dma_start(out_d[4 * j + k], fo[:, k, :]).then_inc(out_done[k], 16)
            for k in range(4):
                sp.wait_ge(out_done[k], 16 * NT // 4 + ONE)
                settle(sp, sp_passed)

        @block.tensor
        def _(pe):
            start_counters(pe, [*scores_done, s["pv"], auxa_full, auxb_full, y_mm])
            pe.wait_ge(silu_done, 1)
            pe.wait_ge(mod_in, 48)
            banks = [XA, XB, Z]
            for k in range(3):
                for c, w in enumerate((wmod, wmod2)):
                    last = pe.matmul(banks[k][0:B, 0:HALF], sc[:, c * B:(c + 1) * B], w[:, k * HALF:(k + 1) * HALF],
                                     start=(c == 0), stop=(c == NC - 1))
            last.then_inc(mod_mm, 1)
            pe.wait_ge(mod_rows, 6)
            pe.wait_ge(consts, 5)
            pe.wait_ge(const_in, 80)

            def step(st):
                g, pp, ap = st.g, st.pp, st.att_par
                used = {"a": 0, "b": 0}

                def aux(which):
                    bank, free, name = (XA, auxa_free, "auxa") if which == "a" else (XB, auxb_free, "auxb")
                    pe.wait_ge(free, st.of(name, used[which]))
                    used[which] += 1
                    return bank

                def project(kind, half):
                    bank = aux("b" if half == 0 else "a")
                    if kind == "q" and half == 0:
                        pe.wait_ge(s["wsplit"], st.of("wsplit", 1))
                        pe.wait_ge(auxa_free, st.n("auxa"))
                    terms = ((Wh, hTh), (Wh, hTl), (Wl, hTh))
                    if kind in "qk":
                        col = 0 if kind == "q" else P
                        for c in range(NC):
                            for n, (w, x) in enumerate(terms):
                                last = pe.matmul(bank[:, :], w[:, pp, c * QKV + col:c * QKV + col + P],
                                                 x[:, st.b % 2, c, half * HALF:(half + 1) * HALF],
                                                 start=(c == 0 and n == 0), stop=(c == NC - 1 and n == 2))
                    else:
                        for t in range(4):
                            tok = (4 * half + t) * P
                            for c in range(NC):
                                for n, (w, x) in enumerate(((Wh, hTh), (Wl, hTh), (Wh, hTl))):
                                    last = pe.matmul(bank[:, t * P:(t + 1) * P], x[:, st.b % 2, c, tok:tok + P],
                                                     w[:, pp, c * QKV + 2 * P:(c + 1) * QKV],
                                                     start=(c == 0 and n == 0), stop=(c == NC - 1 and n == 2))
                    last.then_inc(auxb_full if half == 0 else auxa_full, 1)

                def score(kb, h):
                    pe.wait_ge(exp_done[h], st.of("expd", kb if kb <= 4 else kb - 1))
                    if kb == 0:
                        pe.wait_ge(qk_in[ap], qk_count(st))
                    lo = kb * P
                    spans = [(lo, HALF), (HALF, S)] if lo < HALF else [(lo, S)]
                    for a, z in spans:
                        at = a if kb < 4 else a - HALF + (kb % 2) * HALF
                        for part in range(2):
                            last = pe.matmul(SC[h][:, at:at + z - a], KS[:, ap, h, part, lo:lo + P],
                                             QS[:, ap, h, a:z], start=(part == 0), stop=(part == 1))
                    last.then_inc(scores_done[h], 1)

                def weigh(kb):
                    if kb == 0:
                        pe.wait_ge(s["zevac"], st.n("zevac"))
                    pe.wait_ge(s["vscaled"], st.of("vscaled", kb + 1))
                    lo = kb * P
                    spans = [(lo, HALF), (HALF, S)] if lo < HALF else [(lo, S)]
                    for a, z in spans:
                        for h in range(2):
                            last = pe.matmul(Z[DH * h:DH * h + DH, a:z], vs[:, kb % 2, DH * h:DH * h + DH],
                                             E[:, h, kb % 2, a:z], start=(kb == 0),
                                             stop=(kb == (3 if z == HALF else TPB - 1)))
                    last.then_inc(s["pv"], 1)

                def transpose_tile(x, which, ready):
                    bank = aux(which)
                    pe.wait_ge(s[ready], st.of(ready, 1))
                    for c in range(NC):
                        last = pe.transpose(bank[:, c * P:(c + 1) * P], x[:, c * P:(c + 1) * P], ident[:, :])
                    last.then_inc(auxa_full if which == "a" else auxb_full, 1)

                for kb in range(TPB):
                    if st.has("att"):
                        score(kb, 0)
                        score(kb, 1)
                        if kb >= 1:
                            weigh(kb - 1)
                    if st.has("post") and kb == 0:
                        bank = aux("a")
                        pe.wait_ge(zx_in[pp], zx_count(st))
                        for c in range(PAIRS):
                            last = pe.matmul(bank[:, 0:D], zt[:, pp, c, :], woT[:, c, :], start=(c == 0), stop=(c == PAIRS - 1))
                        last.then_inc(auxa_full, 1)
                    if st.has("proj") and kb in PROJECTIONS:
                        project(*PROJECTIONS[kb])
                    if st.has("post") and kb == 6:
                        transpose_tile(h2[:, pp, :], "b", "h2")
                    if kb == 7:
                        if st.has("post"):
                            bank = aux("b")
                            for c in range(NC):
                                last = pe.matmul(bank[:, 0:NE], h2T[:, c, :], wg[:, c, :], start=(c == 0), stop=(c == NC - 1))
                            last.then_inc(auxb_full, 1)
                        if st.has("ln"):
                            transpose_tile(hn, "a", "hn")
                if st.has("att"):
                    weigh(TPB - 1)

            run_steps(pe, step)

            pe.wait_ge(onehot, 1)
            pe.wait_ge(moe_const, 5)
            flat = oh[:, :, :].rearrange("p t e -> p (t e)")
            pe.matmul(XA[:, :], tri[:, :], flat, start=True, stop=True)
            pe.matmul(XB[:, :], ones[:, :], flat, start=True, stop=True).then_inc(prefix_mm, 1)
            pe.wait_ge(routed, 1)

            xbT = [XA, XB]
            hid = [SC[0][:, 0:HALF], SC[0][:, HALF:S], SC[1][:, 0:HALF], SC[1][:, HALF:S]]
            yps = [Z[:, 0:HALF], Z[:, HALF:S]]

            def expert(e, j, pp, more):
                pe.wait_ge(we_in[pp], 64 * (j + 1))
                pe.wait_ge(bT_done, e + 1)
                for m in range(4):
                    pe.wait_ge(hid_done[m], e + ONE)
                    for half in range(2):
                        for c in range(NC):
                            col = (2 * m + half) * P
                            last = pe.matmul(hid[m][:, half * CAP:(half + 1) * CAP], W1[:, pp, c, col:col + P],
                                             bT[:, pp, c, :], start=(c == 0), stop=(c == NC - 1))
                    last.then_inc(hid_mm[m], 1)
                if more:
                    transpose_rows_at(e + 1, j if pp == 0 else j + 1, 1 - pp)
                pe.wait_ge(y_done, e + ONE)
                for m in range(4):
                    pe.wait_ge(hid_done[m], e + 1 + ONE)
                for i in range(2):
                    for m in range(NM):
                        last = pe.matmul(yps[pp][:, i * D:(i + 1) * D], hh[:, m, i * P:(i + 1) * P], W2[:, pp, m, :],
                                         start=(m == 0), stop=(m == NM - 1))
                last.then_inc(y_mm, 1)

            def transpose_rows_at(e, j, pp):
                pe.wait_ge(bT_done, e)
                pe.wait_ge(xb_in[pp], 16 * (j + 1))
                for c in range(NC):
                    for i in range(2):
                        last = pe.transpose(xbT[pp][:, c * CAP + i * P:c * CAP + (i + 1) * P],
                                            xb[:, pp, i, c * P:(c + 1) * P], ident[:, :])
                last.then_inc(xbT_mm, 1)

            transpose_rows_at(0, 0, 0)
            with pe.Fori(0, NE // 2 - 1) as j:
                for pp in range(2):
                    expert(2 * j + pp, j, pp, True)
            expert(NE - 2, NE // 2 - 1, 0, True)
            expert(NE - 1, NE // 2 - 1, 1, False)

        @block.scalar
        def _(act):
            start_counters(act, [*exp_done, auxb_free, s["zevac"], s["hi"], s["ss"], s["hThi"], hid_done[0], hid_done[2]])
            act.wait_ge(mod_in, 48)
            act.activation(ec[:, :], cT[:, :], ACT.Exp, scale=-1.0).then_inc(c_exp, 1)

            def step(st):
                pp, ap = st.pp, st.att_par
                for kb in range(TPB):
                    if st.has("att"):
                        lo = kb * P
                        at = lo if kb < 4 else lo - HALF + (kb % 2) * HALF
                        for h in range(2):
                            if h == 0:
                                act.wait_ge(s["pv"], st.of("pv", kb - 1 if kb else 0))
                            act.wait_ge(negmax_done[h], st.of("negmax", kb + 1))
                            act.activation(E[:, h, kb % 2, lo:S], SC[h][:, at:at + S - lo], ACT.Exp,
                                           bias=nm[:, h, kb:kb + 1], scale=-1.0,
                                           accum_out=rs[:, kb, h:h + 1]).then_inc(exp_done[h], 1)
                    if st.has("ln") and kb == 3:
                        act.wait_ge(s["h"], st.of("h", 1))
                        act.activation(hsq[:, :], ha[:, :], ACT.Square, accum_out=lss[:, :]).then_inc(s["ss"], 1)
                    if st.has("proj") and kb < 4:
                        kind, half = PROJECTIONS[kb]
                        bank, full, at_ = ((XB, auxb_full, st.of("auxb", 1 + (kind == "k"))) if half == 0 else
                                           (XA, auxa_full, st.of("auxa", st.has("post") + 1 + (kind == "k"))))
                        act.wait_ge(full, at_)
                        if kb == 0:
                            act.wait_ge(s["wsplit"], st.of("wsplit", 1))
                            act.wait_ge(qk_in[1 - pp], qk_count(st))
                        x, k = (XQ, 0) if kind == "q" else (XK, 1)
                        act.activation(x[:, 0, half * HALF:(half + 1) * HALF], bank[:, :], ACT.Identity,
                                       bias=qkb[:, pp, k:k + 1], scale=-1.0 if k else 1.0).then_inc(s["hi"], 1)
                    if st.has("post") and kb == 6:
                        act.wait_ge(auxb_full, st.of("auxb", 3 * st.has("proj") + 1))
                        act.activation(h2T[:, :, :], XB[:, 0:D].rearrange("p (c t) -> p c t", c=NC), ACT.Copy).then_inc(auxb_free, 1)
                    if st.has("ln") and kb == 7:
                        act.wait_ge(auxa_full, st.of("auxa", st.has("post") + 3 * st.has("proj") + 1))
                        act.activation(hTh[:, (st.b + 1) % 2, :, bass.ds(st.i * P, P)],
                                       XA[:, 0:D].rearrange("p (c t) -> p c t", c=NC), ACT.Copy).then_inc(s["hThi"], 1)
                if st.has("att"):
                    act.wait_ge(s["pv"], st.of("pv", TPB))
                    act.wait_ge(z_out, 16 * st.g)
                    act.activation(zs[:, :], Z[:, :], ACT.Copy).then_inc(s["zevac"], 1)
                    act.wait_ge(s["zevac"], st.of("zevac", 1))
                    act.dma_start(z_s[st.g], zs[:, :]).then_inc(z_out, 16)

            run_steps(act, step)

            act.wait_ge(route_exp0, 1)
            act.activation(rb[:, :, :], ra[:, :, :], ACT.Exp).then_inc(route_exp, 1)
            hid = [SC[0][:, 0:HALF], SC[0][:, HALF:S], SC[1][:, 0:HALF], SC[1][:, HALF:S]]
            xbT = [XA, XB]

            def rows(e, pp):
                act.wait_ge(xbT_mm, e + 1)
                act.activation(bT[:, pp, :, :], xbT[pp][:, :].rearrange("p (c t) -> p c t", c=NC), ACT.Copy).then_inc(bT_done, 1)

            rows(0, 0)

            def expert(e, pp, more):
                act.wait_ge(y_mm, e + ONE)
                for m in (0, 2):
                    act.wait_ge(hid_mm[m], e + 1)
                    for half in range(2):
                        last = act.activation(hh[:, 2 * m + half, :], hid[m][:, half * CAP:(half + 1) * CAP], ACT.Relu,
                                              bias=b1t[:, pp, 2 * m + half:2 * m + half + 1])
                    last.then_inc(hid_done[m], 1)
                if more:
                    rows(e + 1, 1 - pp)

            with act.Fori(0, NE // 2 - 1) as j:
                for pp in range(2):
                    expert(2 * j + pp, pp, True)
            expert(NE - 2, 0, True)
            expert(NE - 1, 1, False)

        @block.vector
        def _(dve):
            start_counters(dve, [*negmax_done, auxa_free, hid_done[1], hid_done[3], y_done, scaled, summed])
            start_counters(dve, [s[n] for n in ("vscaled", "rowinv", "xn", "lnve", "ms", "hn", "pve", "xn2", "dlink")])
            dve.wait_ge(c_exp, 1)
            dve.tensor_scalar(ec[:, :], ec[:, :], 1.0, None, ALU.add).then_inc(setup, 1)
            dve.wait_ge(setup, 1)
            dve.reciprocal(sc[:, :], ec[:, :]).then_inc(setup, 1)
            dve.wait_ge(setup, 2)
            dve.tensor_tensor(sc[:, :], sc[:, :], cT[:, :], ALU.mult).then_inc(silu_done, 1)
            dve.memset(mhalf[:, :], -0.5).then_inc(consts, 1)
            dve.wait_ge(mod_mm, 1)
            for k in range(6):
                src = [XA, XB, Z][k // 2][0:B, (k % 2) * D:(k % 2 + 1) * D]
                dst = modr[:, k * D:(k + 1) * D]
                if k in (SA, SB):
                    dve.tensor_copy(dst, src).then_inc(mod_rows, 1)
                elif k in (CA, CB):
                    dve.tensor_scalar(dst, src, 1.0, None, ALU.add).then_inc(mod_rows, 1)
                else:
                    n = 2 + 4 * (k == GB)
                    dve.wait_ge(mod_rows, k)
                    dve.tensor_scalar(sgn[:, 0, :], src, 0.0, 2.0, ALU.is_ge, ALU.mult).then_inc(setup, 1)
                    dve.wait_ge(setup, n + 1)
                    dve.tensor_scalar(sgn[:, 0, :], sgn[:, 0, :], -1.0, None, ALU.add).then_inc(setup, 1)
                    dve.tensor_scalar(sgn[:, 1, :], src, -1.0, 0.25, ALU.mult, ALU.max).then_inc(setup, 1)
                    dve.wait_ge(setup, n + 3)
                    dve.scalar_tensor_tensor(sgn[:, 1, :], src, 0.25, sgn[:, 1, :], ALU.max, ALU.max).then_inc(setup, 1)
                    dve.wait_ge(setup, n + 4)
                    dve.tensor_tensor(dst, sgn[:, 0, :], sgn[:, 1, :], ALU.mult).then_inc(mod_rows, 1)

            dve.wait_ge(consts, 5)
            dve.wait_ge(const_in, 80)

            def step(st):
                pp, ap = st.pp, st.att_par
                links = [0]

                def link(ins):
                    links[0] += 1
                    ins.then_inc(s["dlink"], 1)
                    dve.wait_ge(s["dlink"], st.of("dlink", links[0]))

                def stats(x, stt, mv, ve):
                    link(dve.bn_stats(stt[:, :], x))
                    settle(dve, dve_passed)
                    link(dve.bn_aggr(mv[:, :], stt[:, :]))
                    return dve.tensor_scalar(ve[:, :], mv[:, 1:2], LN_EPS, None, ALU.add)

                def scale_values(kb):
                    if kb == 0:
                        dve.wait_ge(auxa_free, st.n("auxa"))
                        dve.wait_ge(auxb_free, st.n("auxb"))
                    for h in range(2):
                        dve.wait_ge(exp_done[h], st.of("expd", kb + 1))
                    dve.reciprocal(ri[:, kb % 2, :], rs[:, kb, :]).then_inc(s["rowinv"], 1)
                    if kb >= 2:
                        dve.wait_ge(s["pv"], st.of("pv", kb - 1))
                    else:
                        dve.wait_ge(s["pv"], st.n("pv"))
                    dve.wait_ge(s["rowinv"], st.of("rowinv", kb + 1))
                    dve.tensor_tensor(vs[:, kb % 2, :].rearrange("p (h d) -> p h d", h=2),
                                      V[:, ap, kb, :].rearrange("p (h d) -> p h d", h=2),
                                      ri[:, kb % 2, :].unsqueeze(2).broadcast_to([P, 2, DH]), ALU.mult).then_inc(s["vscaled"], 1)

                for kb in range(TPB):
                    if st.has("att"):
                        lo = kb * P
                        at = lo if kb < 4 else lo - HALF + (kb % 2) * HALF
                        for h in range(2):
                            dve.wait_ge(scores_done[h], st.of("scores", kb + 1))
                            settle(dve, dve_passed)
                            dve.tensor_tensor_reduce(SC[h][:, at:at + S - lo], SC[h][:, at:at + S - lo], mask[:, 0:S - lo],
                                                     1.0, BIG, ALU.add, ALU.min, nm[:, h, kb:kb + 1]).then_inc(negmax_done[h], 1)
                    if st.has("post") and kb == 1:
                        dve.wait_ge(auxa_full, st.of("auxa", 1))
                        dve.wait_ge(s["x1"], st.n("x1"))
                        dve.tensor_tensor(pt[:, :], XA[:, 0:D], boB[:, :], ALU.add).then_inc(auxa_free, 1)
                    if st.has("proj") and 1 <= kb <= 4:
                        n = kb - 1
                        kind, half = PROJECTIONS[n]
                        cols = slice(half * HALF, (half + 1) * HALF)
                        dve.wait_ge(s["hi"], st.of("hi", n + 1))
                        bank, free = (XB, auxb_free) if half == 0 else (XA, auxa_free)
                        if kind == "q":
                            last = dve.scalar_tensor_tensor(XQ[:, 1, cols], bank[:, :], qkb[:, pp, 0:1],
                                                            XQ[:, 0, cols].bitcast(F32), ALU.add, ALU.subtract)
                        else:
                            last = dve.scalar_tensor_tensor(XK[:, 1, cols], bank[:, :], qkb[:, pp, 1:2],
                                                            XK[:, 0, cols].bitcast(F32), ALU.subtract, ALU.subtract,
                                                            reverse0=True)
                        last.then_inc(free, 1)
                    if st.has("proj") and kb in (5, 7):
                        half = int(kb == 7)
                        full, at_, free, bank = ((auxb_full, st.of("auxb", 3), auxb_free, XB) if half == 0 else
                                                 (auxa_full, st.of("auxa", st.has("post") + 3), auxa_free, XA))
                        dve.wait_ge(full, at_)
                        dve.tensor_tensor(V[:, st.proj_par, 4 * half:4 * half + 4, :],
                                          bank[:, :].rearrange("p (t d) -> p t d", t=4),
                                          bvB[:, bass.ds(st.i * P, P)].unsqueeze(1).broadcast_to([P, 4, P]), ALU.add)\
                            .then_inc(free, 1)
                    if st.has("ln"):
                        if kb == 0:
                            dve.wait_ge(xln_in[pp], 16 * ((st.b + 1) * PAIRS // 2 + st.j + 1))
                            stats(xln[:, pp, :], lst, lmv, lve).then_inc(s["lnve"], 1)
                        if kb == 1:
                            dve.wait_ge(s["rstd"], st.of("rstd", 1))
                            dve.wait_ge(s["h"], st.n("h"))
                            dve.tensor_scalar(xnb[:, :], xln[:, pp, :], lmv[:, 0:1], lrs[:, :], ALU.subtract,
                                              ALU.mult).then_inc(s["xn"], 1)
                        if kb == 4:
                            dve.wait_ge(s["ss"], st.of("ss", 1))
                            dve.tensor_scalar(lms[:, :], lss[:, :], 1.0 / D, RMS_EPS, ALU.mult, ALU.add).then_inc(s["ms"], 1)
                        if kb == 6:
                            dve.wait_ge(s["rr"], st.of("rr", 1))
                            dve.wait_ge(auxa_full, st.n("auxa"))
                            dve.tensor_scalar(hn[:, :], ha[:, :], lrr[:, :], None, ALU.mult).then_inc(s["hn"], 1)
                    if st.has("post"):
                        if kb == 2:
                            dve.wait_ge(s["x1"], st.of("x1", 1))
                            stats(x1[:, pp, :], pst, pmv, pve).then_inc(s["pve"], 1)
                        if kb == 3:
                            dve.wait_ge(s["prstd"], st.of("prstd", 1))
                            dve.wait_ge(s["h2"], st.n("h2"))
                            dve.tensor_scalar(xn2[:, :], x1[:, pp, :], pmv[:, 0:1], prs[:, :], ALU.subtract,
                                              ALU.mult).then_inc(s["xn2"], 1)
                    if st.has("att"):
                        scale_values(kb)
                if st.has("post"):
                    dve.wait_ge(auxb_full, st.of("auxb", 3 * st.has("proj") + 2))
                    dve.tensor_tensor(logits[:, bass.ds(st.tile, 1), :], XB[:, 0:NE].unsqueeze(1), bgB[:, :].unsqueeze(1), ALU.add)\
                        .then_inc(auxb_free, 1)
                if st.has("ln"):
                    dve.wait_ge(s["hThi"], st.of("hThi", 1))
                    cols = bass.ds(st.i * P, P)
                    dve.tensor_tensor(hTl[:, (st.b + 1) % 2, :, cols], XA[:, 0:D].rearrange("p (c t) -> p c t", c=NC),
                                      hTh[:, (st.b + 1) % 2, :, cols].bitcast(F32), ALU.subtract).then_inc(auxa_free, 1)
                assert links[0] == sum(v for k, v in RISES["dlink"].items() if st.has(k))

            run_steps(dve, step)

            steps = [0]

            def link(ins):
                steps[0] += 1
                ins.then_inc(route, 1)
                dve.wait_ge(route, steps[0])

            def wide(a):
                return a.unsqueeze(2).broadcast_to([P, NT, NE])

            def each(a):
                return a.unsqueeze(1).broadcast_to([P, NT, NE])

            dve.wait_ge(auxb_free, TOTAL["auxb"])
            dve.wait_ge(moe_const, 5)
            link(dve.tensor_reduce(r1[:, :], logits[:, :, :], AX.X, ALU.max))
            dve.tensor_tensor(ra[:, :, :], logits[:, :, :], wide(r1[:, :]), ALU.subtract).then_inc(route_exp0, 1)
            dve.wait_ge(route_exp0, 1)
            link(dve.tensor_scalar(rc[:, :, :], ra[:, :, :], 0.0, None, ALU.is_ge))
            link(dve.tensor_tensor(rc[:, :, :], rc[:, :, :], each(revj[:, :]), ALU.mult))
            link(dve.tensor_reduce(r2[:, :], rc[:, :, :], AX.X, ALU.max))
            dve.tensor_tensor(oh[:, :, :], rc[:, :, :], wide(r2[:, :]), ALU.is_equal).then_inc(onehot, 1)
            dve.wait_ge(route_exp, 1)
            link(dve.tensor_reduce(r3[:, :], rb[:, :, :], AX.X, ALU.add))
            link(dve.reciprocal(r3[:, :], r3[:, :]))
            dve.wait_ge(onehot, 1)
            link(dve.tensor_tensor(rc[:, :, :], oh[:, :, :], each(ebase[:, :]), ALU.mult))
            link(dve.tensor_reduce(r4[:, :], rc[:, :, :], AX.X, ALU.add))
            dve.wait_ge(prefix_mm, 1)
            link(dve.memset(base[:, 0, :], 0.0))
            tot = XB[:, :].rearrange("p (t e) -> p t e", t=NT)
            for t in range(1, NT):
                link(dve.tensor_tensor(base[:, t, :], base[:, t - 1, :], tot[:, t - 1, :], ALU.add))
            link(dve.tensor_tensor(ra[:, :, :], XA[:, :].rearrange("p (t e) -> p t e", t=NT), base[:, :, :], ALU.add))
            link(dve.tensor_tensor(ra[:, :, :], ra[:, :, :], oh[:, :, :], ALU.mult))
            link(dve.tensor_reduce(r1[:, :], ra[:, :, :], AX.X, ALU.add))
            link(dve.tensor_scalar(keepm[:, :], r1[:, :], float(CAP), None, ALU.is_lt))
            link(dve.tensor_tensor(gates[:, :], r3[:, :], keepm[:, :], ALU.mult))
            link(dve.tensor_tensor(r1[:, :], r1[:, :], r4[:, :], ALU.add))
            link(dve.tensor_scalar(r2[:, :], keepm[:, :], -FAR, FAR, ALU.mult, ALU.add))
            dve.tensor_tensor(slot_u[:, :], r1[:, :], r2[:, :], ALU.add).then_inc(routed, 1)

            hid = [SC[0][:, 0:HALF], SC[0][:, HALF:S], SC[1][:, 0:HALF], SC[1][:, HALF:S]]

            def expert(e, j, pp):
                dve.wait_ge(y_mm, e + ONE)
                for m in (1, 3):
                    dve.wait_ge(hid_mm[m], e + 1)
                    for half in range(2):
                        last = dve.tensor_scalar(hh[:, 2 * m + half, :], hid[m][:, half * CAP:(half + 1) * CAP],
                                                 b1t[:, pp, 2 * m + half:2 * m + half + 1], 0.0, ALU.add, ALU.max)
                    last.then_inc(hid_done[m], 1)
                dve.wait_ge(y_mm, e + 1 + ONE)
                dve.wait_ge(y_out[pp], 16 * j + ONE)
                dve.tensor_tensor(yb[:, pp, :, :], Z[:, pp * HALF:(pp + 1) * HALF].rearrange("p (i d) -> p i d", i=2),
                                  b2B[:, pp, :].unsqueeze(1).broadcast_to([P, 2, D]), ALU.add).then_inc(y_done, 1)

            with dve.Fori(0, NE // 2) as j:
                for pp in range(2):
                    expert(2 * j + pp, j, pp)

            with dve.Fori(0, NT // 4) as j:
                for k in range(4):
                    t = 4 * j + k
                    dve.wait_ge(gat_in[k], 16 * (j + 1))
                    dve.wait_ge(summed, 4 * j + max(0, k - 1) + ONE)
                    dve.scalar_tensor_tensor(ft[:, k % 2, :], gat[:, k, :], gcol[:, k:k + 1], modB[:, t // TPB, GB, :],
                                             ALU.mult, ALU.mult).then_inc(scaled, 1)
                    dve.wait_ge(scaled, t + 1 + ONE)
                    dve.wait_ge(fx_in[k], 16 * (j + 1))
                    dve.wait_ge(out_done[k], 16 * j + ONE)
                    dve.tensor_tensor(fo[:, k, :], ft[:, k % 2, :], fx[:, k, :], ALU.add).then_inc(summed, 1)

        @block.gpsimd
        def _(pool):
            start_counters(pool, [s[n] for n in ("rstd", "h", "rr", "x1", "prstd", "h2", "plink", "wsplit")])
            pool.memset(ident[:, :], 0.0).then_inc(consts, 1)
            pool.memset(mask[:, :], 0.0).then_inc(consts, 1)
            pool.wait_ge(consts, 3)
            pool.affine_select(ident[:, :], ident[:, :], pattern=[[-1, P]], compare_op=ALU.not_equal, fill=1.0,
                               base=0, channel_multiplier=1).then_inc(consts, 1)
            pool.affine_select(mask[:, 0:P], mask[:, 0:P], pattern=[[1, P]], compare_op=ALU.is_ge, fill=BIG,
                               base=0, channel_multiplier=-1).then_inc(consts, 1)
            pool.wait_ge(modb_in, 16)

            def split_weights(par):
                pool.tensor_copy(qkb[:, par, 0:1], W[:, WROW - 2:WROW - 1])
                pool.tensor_scalar(qkb[:, par, 1:2], W[:, WROW - 1:WROW], -1.0, None, ALU.mult)
                return pool.tensor_copy(Wh[:, par, :], W[:, 0:NC * QKV])

            def last_split(par):
                return pool.tensor_tensor(Wl[:, par, :], W[:, 0:NC * QKV], Wh[:, par, :].bitcast(F32), ALU.subtract)

            def step(st):
                pp = st.pp
                links = [0]

                def link(ins):
                    links[0] += 1
                    ins.then_inc(s["plink"], 1)
                    pool.wait_ge(s["plink"], st.of("plink", links[0]))

                if st.has("ln"):
                    pool.wait_ge(s["lnve"], st.of("lnve", 1))
                    pool.tensor_tensor(lrs[:, :], lve[:, :], mhalf[:, :], ALU.pow).then_inc(s["rstd"], 1)
                    pool.wait_ge(s["xn"], st.of("xn", 1))
                    pool.wait_ge(s["hn"], st.n("hn"))
                    link(pool.tensor_tensor(ha[:, :], xnb[:, :], modB[:, st.b + 1, CA, :], ALU.mult))
                    pool.tensor_tensor(ha[:, :], ha[:, :], modB[:, st.b + 1, SA, :], ALU.add).then_inc(s["h"], 1)
                if st.has("post"):
                    bt = st.tile // TPB
                    pool.wait_ge(auxa_free, st.of("auxa", 1))
                    link(pool.tensor_tensor(pt[:, :].unsqueeze(1), pt[:, :].unsqueeze(1), modB[:, bass.ds(bt, 1), GA, :], ALU.mult))
                    pool.wait_ge(zx_in[pp], zx_count(st))
                    pool.wait_ge(post_out[pp], zx_count(st) - 32 + ONE)
                    pool.tensor_tensor(x1[:, pp, :], pt[:, :], xp[:, pp, :], ALU.add).then_inc(s["x1"], 1)
                    pool.wait_ge(s["pve"], st.of("pve", 1))
                    pool.tensor_tensor(prs[:, :], pve[:, :], mhalf[:, :], ALU.pow).then_inc(s["prstd"], 1)
                    pool.wait_ge(s["xn2"], st.of("xn2", 1))
                    link(pool.tensor_tensor(h2[:, pp, :].unsqueeze(1), xn2[:, :].unsqueeze(1), modB[:, bass.ds(bt, 1), CB, :], ALU.mult))
                    pool.tensor_tensor(h2[:, pp, :].unsqueeze(1), h2[:, pp, :].unsqueeze(1), modB[:, bass.ds(bt, 1), SB, :], ALU.add).then_inc(s["h2"], 1)
                if st.has("ln"):
                    pool.wait_ge(s["ms"], st.of("ms", 1))
                    pool.tensor_tensor(lrr[:, :], lms[:, :], mhalf[:, :], ALU.pow).then_inc(s["rr"], 1)
                if st.has("proj"):
                    pool.wait_ge(w_in, 16 * (st.b * PAIRS + st.i + 2))
                    pool.wait_ge(auxa_full, st.n("auxa"))
                    pool.wait_ge(auxb_full, st.n("auxb"))
                    settle(pool, pool_passed)
                    link(split_weights(1 - pp))
                    last_split(1 - pp).then_inc(s["wsplit"], 1)

            pool.wait_ge(w_in, 16)
            split_weights(0).then_inc(setup_split, 1)
            pool.wait_ge(setup_split, 1)
            last_split(0).then_inc(s["wsplit"], 1)

            run_steps(pool, step)

            pool.wait_ge(s["zevac"], TOTAL["zevac"])
            pool.wait_ge(z_out, 16 * NG)
            pool.memset(zero[:, :], 0.0).then_inc(moe_const, 1)
            pool.memset(ones[:, :], 1.0).then_inc(moe_const, 1)
            pool.wait_ge(moe_const, 2)
            pool.affine_select(tri[:, :], ones[:, :], pattern=[[1, P]], compare_op=ALU.is_gt, fill=0.0,
                               base=0, channel_multiplier=-1).then_inc(moe_const, 1)
            pool.iota(revj[:, :], pattern=[[-1, NE]], base=NE, channel_multiplier=0,
                      allow_small_or_imprecise_dtypes=True).then_inc(moe_const, 1)
            pool.iota(ebase[:, :], pattern=[[CAP, NE]], base=0, channel_multiplier=0,
                      allow_small_or_imprecise_dtypes=True).then_inc(moe_const, 1)
            pool.wait_ge(routed, 1)
            pool.wait_ge(zeroed, 16 * (NE * CAP // P // 2))

            def scatter(j):
                for k in range(4):
                    if not isinstance(j, int):
                        pool.wait_ge(scattered[k], 16 * j)
                    pool.tensor_copy(idx[:, k:k + 1], slot_u[:, bass.ds(4 * j + k, 1)]).then_inc(idx_ok, 1)
                    pool.wait_ge(idx_ok, 4 * j + k + 1)
                    pool.wait_ge(hs_in[k], 16 * (j + 1))
                    settle(pool, pool_passed)
                    pool.indirect_dma_start(slots_s, bass.IndirectOffsetOnAxis(idx[:, k:k + 1], 0), hs[:, k, :], None,
                                            bounds_check=NE * CAP - 1, oob_is_err=False).then_inc(scattered[k], 16)

            scatter(0)
            with pool.Fori(1, NT // 4) as j:
                scatter(j)
            for k in range(4):
                pool.wait_ge(scattered[k], 16 * (NT // 4))
            for pp in range(2):
                pool.wait_ge(y_out[pp], 16 * NE // 2 + ONE)
            with pool.Fori(0, NT // 4) as j:
                for k in range(4):
                    pool.wait_ge(scaled, 4 * j + ONE)
                    pool.tensor_copy(idx[:, k:k + 1], slot_u[:, bass.ds(4 * j + k, 1)]).then_inc(idx_ok, 1)
                    pool.tensor_copy(gcol[:, k:k + 1], gates[:, bass.ds(4 * j + k, 1)]).then_inc(gat_clear, 1)
                    pool.memset(gat[:, k, :], 0.0).then_inc(gat_clear, 1)
                    pool.wait_ge(idx_ok, NT + 4 * j + k + 1)
                    pool.wait_ge(gat_clear, 8 * j + 2 * k + 2)
                    settle(pool, pool_passed)
                    pool.indirect_dma_start(gat[:, k, :], None, y_s, bass.IndirectOffsetOnAxis(idx[:, k:k + 1], 0),
                                            bounds_check=NE * CAP - 1, oob_is_err=False).then_inc(gat_in[k], 16)


def kernel(**inputs):
    import numpy as np
    import concourse.bacc as bacc
    from concourse.bass_utils import run_bass_kernel_spmd

    a = {k: np.asarray(v) for k, v in inputs.items()}
    w = a["L0_attn_W_qkv"].reshape(PAIRS, 2, DH, 3, NC, P).transpose(0, 5, 4, 3, 1, 2).reshape(PAIRS, P, NC * QKV)
    bqkv = a["L0_attn_b_qkv"].reshape(PAIRS, P, 3)
    arrays = {
        "x": a["L0_attn_x"].reshape(NT, P, D),
        "wqkv": np.concatenate([w, bqkv[:, :, 0:2]], axis=2),
        "bv": bqkv[:, :, 2].reshape(1, PAIRS * P),
        "wo": a["L0_attn_W_o"].T.reshape(PAIRS, P, D).transpose(1, 0, 2),
        "bo": a["L0_attn_b_o"].reshape(1, D),
        "wg": a["L0_ffn_Wg"].reshape(NC, P, NE).transpose(1, 0, 2),
        "bg": a["L0_ffn_bg"].reshape(1, NE),
        "w1": a["L0_ffn_W1"],
        "b1": a["L0_ffn_b1"].reshape(NE, NM, P).transpose(0, 2, 1),
        "w2": a["L0_ffn_W2"],
        "b2": a["L0_ffn_b2"],
        "c": a["L0_c"].reshape(B, NC, P).transpose(2, 1, 0).reshape(P, NC * B),
        "wmod": a["L0_wmod"].reshape(NC, P, 6 * D),
    }
    nc = bacc.Bacc("TRN2", target_bir_lowering=False, num_devices=1)
    feeds, args = {}, []
    for name, v in arrays.items():
        v = np.ascontiguousarray(v)
        feeds[f"in_{name}"] = v
        args.append(nc.dram_tensor(f"in_{name}", v.shape, mybir.dt.from_np(v.dtype), kind="ExternalInput").ap())
    args.append(nc.dram_tensor("out", [NT, P, D], F32, kind="ExternalOutput").ap())
    adaln_block(nc, *args)
    r = run_bass_kernel_spmd(nc, [feeds], core_ids=[0])
    return r.results[0]["out"].reshape(B, S, D)
```

```python
from contextlib import ExitStack

import concourse.bass as bass
from concourse import mybir

P = 128
B, S, D = 4, 1024, 256
H, DH = 16, 64
PAIRS = H // 2
NG = B * PAIRS
TPB = S // P
NT = B * TPB
NC = D // P
NE, HID = 16, 1024
NM = HID // P
CAP = B * S // NE
HALF = 512
LAG = PAIRS + 1
QK = 2 * P
CV = 2 * P
COUPLES = PAIRS // 2
LN_EPS = 1e-5
RMS_EPS = 1.1920929e-07
BIG = 3.0e38
FAR = float(1 << 20)
ROW = 2 * D + 8
TOKEN, GATE = 2 * D, 2 * D + 1
NW = 4
HS = 8
TAIL = TPB + 1
T0 = NT - TAIL
GROUPS = [(0, 1)] + [(1 + 2 * k, 2) for k in range(TPB // 2)]
LOTS = [(0, 2 * TPB), (2 * TPB, 3 * TPB), (3 * TPB, NT)]
FILL = 2
FILLS = NE * CAP // P // FILL


ALU = mybir.AluOpType
ACT = mybir.ActivationFunctionType
AX = mybir.AxisListType
F32 = mybir.dt.float32
F32R = mybir.dt.float32r
U32 = mybir.dt.uint32

ONE = 1

SA, CA, GA, SB, CB, GB = range(6)

RISES = {
    "scores": dict(att=TPB), "negmax": dict(att=TPB), "expd": dict(att=TPB), "vscaled": dict(att=TPB),
    "rowinv": dict(att=TPB), "pv": dict(att=TPB), "zevac": dict(att=1),
    "auxa": dict(post=1, proj=3, ln=1), "auxb": dict(proj=3, post=2),
    "hi": dict(proj=4), "wsplit": dict(proj=1), "hThi": dict(ln=1),
    "xn": dict(ln=1), "lnve": dict(ln=1), "rstd": dict(ln=1), "h": dict(ln=1), "ss": dict(ln=1), "ms": dict(ln=1),
    "rr": dict(ln=1), "hn": dict(ln=1),
    "x1": dict(post=1), "pve": dict(post=1), "prstd": dict(post=1), "xn2": dict(post=1),
    "h2": dict(post=1),
    "dlink": dict(ln=2, post=2), "plink": dict(ln=1, post=2, proj=1),
}


class Step:

    def __init__(self, seg, b, j, pp, before, since):
        self.seg, self.b, self.j, self.pp, self.before, self.since = seg, b, j, pp, before, since
        self.i = 2 * j + pp
        self.g = b * PAIRS - 1 + self.i
        self.tile = self.g - LAG
        self.att_par, self.proj_par = 1 - pp, pp

    def has(self, part):
        return part in self.seg

    def n(self, name):
        per = sum(v for k, v in RISES[name].items() if k in self.seg)
        return self.before[name] + per * self.since

    def of(self, name, k):
        return self.n(name) + k


PIECES = [
    {0: [("q", 0)], 1: [("q", 1)], 2: [("k", 0)], 3: [("k", 1)], 4: [("v", 0)], 6: [("v", 1)]},
    {0: [("q", 0)], 1: [("q", 1)], 2: [("k", 0)], 3: [("k", 1), ("v", 2)], 5: [("v", 3)]},
]


def piece_use(pp, piece):
    order = [p for kb in sorted(PIECES[pp]) for p in PIECES[pp][kb] if p[1] % 2 == piece[1] % 2]
    return order.index(piece) + 1


SEGS = [
    (0, 0, 1, (0,), ("proj", "ln")),
    (0, 0, 1, (1,), ("att", "proj", "ln")),
    (0, 1, 4, (0, 1), ("att", "proj", "ln")),
    (1, 0, 1, (0, 1), ("att", "proj", "ln")),
    (1, 1, 4, (0, 1), ("att", "proj", "ln", "post")),
    (2, 0, 4, (0, 1), ("att", "proj", "ln", "post")),
    (3, 0, 4, (0, 1), ("att", "proj", "post")),
    (4, 0, 1, (0,), ("att", "post")),
]


def rises_before(k):
    done = {name: ONE for name in RISES}
    for b, j0, j1, halves, parts in SEGS[:k]:
        steps = (j1 - j0) * len(halves)
        for name, per in RISES.items():
            done[name] += steps * sum(v for part, v in per.items() if part in parts)
    return done


def run_steps(eng, body):
    for k, (b, j0, j1, halves, parts) in enumerate(SEGS):
        before = rises_before(k)
        if j1 - j0 == 1:
            for n, pp in enumerate(halves):
                body(Step(parts, b, j0, pp, before, n))
        else:
            with eng.Fori(j0, j1) as j:
                for pp in halves:
                    body(Step(parts, b, j, pp, before, 2 * (j - j0) + pp))


TOTAL = rises_before(len(SEGS))


def start_counters(eng, sems):
    for x in sems:
        eng.sem_inc(x, ONE)


def settle(eng, passed):
    eng.sem_inc(passed, 1)


def qk_count(st):
    return 12 * 16 * (st.b * PAIRS // 2 + st.j + st.pp)


def zx_count(st):
    return 32 * (st.b * PAIRS // 2 + st.j - (LAG + 1) // 2 + 1)


def run_experts(eng, body):
    for k in range(NW):
        body(0, k)
    with eng.Fori(1, NE // NW - 1) as j:
        for k in range(NW):
            body(j, k)
    for k in range(NW):
        body(NE // NW - 1, k)


def adaln_block(nc, x_d, wqk_d, wv_d, bv_d, wo_d, bo_d, wg_d, bg_d, w1_d, b1_d, w2_d, b2_d, c_d, wmod_d, out_d):
    keep = ExitStack()
    with keep:
        def dram(name, shape, dt=F32):
            return nc.dram_tensor(name, shape, dt, kind="Internal").ap()

        place, top = {}, [0]

        def sb(name, shape, dt=F32, stack=keep):
            place[name] = top[0]
            size = 4
            for n in shape[1:]:
                size *= n
            top[0] += -(-size // 32) * 32
            return stack.enter_context(nc.sbuf_tensor(name, shape, dt))

        def sem(name):
            return keep.enter_context(nc.semaphore(name))

        mod_s = dram("mod_s", [B, 6 * D])
        z_s = dram("z_s", [NG, P, S])
        xh_s = dram("xh_s", [NT, P, 2 * D])
        slots_s = dram("slots_s", [NE * CAP, ROW])

        ident = sb("ident", [P, P])
        modB = sb("modB", [P, B, 6, D])
        logits = sb("logits", [P, NT, NE])
        slot_u = sb("slot_u", [P, NT], U32)
        gates = sb("gates", [P, NT])
        mhalf = sb("mhalf", [P, 1])

        woT = sb("woT", [P, PAIRS, D])
        boB = sb("boB", [P, D])
        wg = sb("wg", [P, NC, NE])
        bgB = sb("bgB", [P, NE])
        zt = sb("zt", [P, 2, PAIRS, P])
        xp = sb("xp", [P, 2, D])
        pt = sb("pt", [P, D])
        x1 = sb("x1", [P, 2, D])
        xn2 = sb("xn2", [P, D])
        h2 = sb("h2", [P, 2, D])
        h2T = sb("h2T", [P, NC, P])
        pst = sb("pst", [P, 6])
        pmv = sb("pmv", [P, 2])
        pve = sb("pve", [P, 1])
        prs = sb("prs", [P, 1])

        att = ExitStack()
        E = sb("E", [P, 2, 2, S], stack=att)
        QS = sb("QS", [P, 2, 2, S], F32R, stack=att)
        KS = sb("KS", [P, 2, 2, 2, S], F32R, stack=att)
        XQ = sb("XQ", [P, 2, S], F32R, stack=att)
        XK = sb("XK", [P, 2, S], F32R, stack=att)
        V = sb("V", [P, TPB, 2, P], stack=att)
        vs = sb("vs", [P, 2, P], stack=att)
        rs = sb("rs", [P, TPB, 2], stack=att)
        ri = sb("ri", [P, 2, 2], stack=att)
        nm = sb("nm", [P, 2, TPB], stack=att)
        mask = sb("mask", [P, S], stack=att)
        hTh = sb("hTh", [P, 2, NC, S], F32R, stack=att)
        hTl = sb("hTl", [P, 2, NC, S], F32R, stack=att)
        W = sb("W", [P, NC * QK + 2], stack=att)
        Wv = sb("Wv", [P, NC * CV], stack=att)
        Wh = sb("Wh", [P, 2, NC * QK], F32R, stack=att)
        Wl = sb("Wl", [P, 2, NC * QK], F32R, stack=att)
        Wvh = sb("Wvh", [P, NC * CV], F32R, stack=att)
        Wvl = sb("Wvl", [P, NC * CV], F32R, stack=att)
        qkb = sb("qkb", [P, 2, 2], stack=att)
        bvB = sb("bvB", [P, PAIRS * P], stack=att)
        zs = sb("zs", [P, S], stack=att)
        xln = sb("xln", [P, 2, D], stack=att)
        xnb = sb("xnb", [P, D], stack=att)
        ha = sb("ha", [P, D], stack=att)
        hn = sb("hn", [P, D], stack=att)
        lst = sb("lst", [P, 6], stack=att)
        lmv = sb("lmv", [P, 2], stack=att)
        lve = sb("lve", [P, 1], stack=att)
        lrs = sb("lrs", [P, 1], stack=att)
        lss = sb("lss", [P, 1], stack=att)
        lms = sb("lms", [P, 1], stack=att)
        lrr = sb("lrr", [P, 1], stack=att)
        wmod = E[:, 0, :, :].rearrange("p a b -> p (a b)")
        wmod2 = E[:, 1, :, :].rearrange("p a b -> p (a b)")
        cT = sb("cT", [P, NC * B], stack=att)
        ec = sb("ec", [P, NC * B], stack=att)
        sc = sb("sc", [P, NC * B], stack=att)
        modr = V[0:B, :, :, :].rearrange("p a b c -> p (a b c)")[:, 0:6 * D]
        sgn = zs[0:B, 0:2 * D].rearrange("p (a d) -> p a d", a=2)
        blank = zt[:, :, :, :].rearrange("p a c t -> p (a c t)")[:, 0:FILL * ROW]
        xw = woT[:, :, :]
        hw = V[:, :, :, :].rearrange("p t a d -> p t (a d)")
        room = E[:, 0, 1, HALF:S]
        wst = room[:, 0:6 * TPB].rearrange("p (t k) -> p t k", t=TPB)
        wmv = room[:, 6 * TPB:8 * TPB].rearrange("p (t k) -> p t k", t=TPB)
        wve, wrs, wss, wms, wrr = (room[:, k * TPB:(k + 1) * TPB] for k in range(8, 13))
        att.close()

        top[0] = place["E"]

        xb = sb("xb", [P, NW, 2, ROW])
        hs = xb[:, :, :, :].rearrange("p a b w -> p (a b) w")
        W1 = sb("W1", [P, NW, NC, HID])
        W2 = sb("W2", [P, NW, NM, D])
        b1t = sb("b1t", [P, NW, NM])
        b2B = sb("b2B", [P, NW, D])
        ra = sb("ra", [P, NT, NE])
        rb = sb("rb", [P, NT, NE])
        rc = sb("rc", [P, NT, NE])
        small = [sb(n, [P, NT]) for n in ("r1", "r2", "r3", "r4", "keepm")]
        r1, r2, r3, r4, keepm = small
        assert top[0] <= place["hTh"]
        zA = hTh[:, :, :, :].bitcast(F32).rearrange("p a c t -> p (a c) t")
        zB = hTl[:, :, :, :].bitcast(F32).rearrange("p a c t -> p (a c) t")
        sb("left_below_z", [P, (place["hTh"] - top[0]) // 4])
        hh = sb("hh", [P, 2, NM, CAP])
        bT = sb("bT", [P, 2, NC, CAP])
        grow = sb("grow", [P, 2, D])
        yb = sb("yb", [P, 2, 2, D])
        assert top[0] <= place["W"]
        sb("left_below_w", [P, (place["W"] - top[0]) // 4])
        th = sb("th", [P, TAIL, ROW])
        ext = sb("ext", [P, NT, ROW - 2 * D])
        assert top[0] <= place["zs"]
        sb("left_zs", [P, (place["xln"] - top[0]) // 4])
        tri = sb("tri", [P, P])
        ones = sb("ones", [P, P])
        revj = sb("revj", [P, NE])
        ebase = sb("ebase", [P, NE])
        oh = sb("oh", [P, NT, NE])
        base = sb("base", [P, NT, NE])
        tok = sb("tok", [P, 2, 2], U32)
        tst = sb("tst", [P, 2, 6])
        tmv = sb("tmv", [P, 2, 2])
        tve = sb("tve", [P, 2])
        trs = sb("trs", [P, 2])
        tT = zt[:, 0, 0:2 * NC, :]
        tp = zt[:, 0, 2 * NC:4 * NC, :].rearrange("p (q c) t -> p q (c t)", q=2)

        SC = [keep.enter_context(nc.psum_tensor(f"SC{h}", [P, S], F32)) for h in range(2)]
        Z = keep.enter_context(nc.psum_tensor("Z", [P, S], F32))
        XA = keep.enter_context(nc.psum_tensor("XA", [P, HALF], F32))
        XB = keep.enter_context(nc.psum_tensor("XB", [P, HALF], F32))

        names = [n for n in RISES if n not in ("scores", "negmax", "expd")]
        s = {n: sem("s_" + n) for n in names}
        scores_done = [sem(f"scores_done{h}") for h in range(2)]
        negmax_done = [sem(f"negmax_done{h}") for h in range(2)]
        exp_done = [sem(f"exp_done{h}") for h in range(2)]
        auxa_full, auxa_free = s["auxa"], sem("auxa_free")
        auxb_full, auxb_free = s["auxb"], sem("auxb_free")
        w_in = sem("w_in")
        wv_in = sem("wv_in")
        wv_lead = sem("wv_lead")
        wv_split = sem("wv_split")
        qk_in = [sem(f"qk_in{k}") for k in range(2)]
        xln_in = [sem(f"xln_in{k}") for k in range(2)]
        zx_in = [sem(f"zx_in{k}") for k in range(2)]
        z_out = sem("z_out")
        post_out = [sem(f"post_out{k}") for k in range(2)]
        const_in = sem("const_in")
        mod_in = sem("mod_in")
        mod_out = sem("mod_out")
        modb_in = sem("modb_in")
        consts = sem("consts")
        c_exp = sem("c_exp")
        setup = sem("setup")
        silu_done = sem("silu_done")
        mod_mm = sem("mod_mm")
        mod_rows = sem("mod_rows")
        setup_split = sem("setup_split")

        wo_in = sem("wo_in")
        xw_in = sem("xw_in")
        modb0_in = sem("modb0_in")
        wide = sem("wide")
        wide_ve = sem("wide_ve")
        wide_rs = sem("wide_rs")
        wide_h = sem("wide_h")
        wide_ss = sem("wide_ss")
        wide_ms = sem("wide_ms")
        wide_rr = sem("wide_rr")
        wide_hn = sem("wide_hn")
        wide_turned = sem("wide_turned")
        wide_hi = sem("wide_hi")
        wide_lo = sem("wide_lo")
        blank_set = sem("blank_set")
        filled = sem("filled")
        moe_const = sem("moe_const")
        route = sem("route")
        tail_z0 = sem("tail_z0")
        tail_z = sem("tail_z")
        tail_x = sem("tail_x")
        tail_wo = sem("tail_wo")
        tail_ve = sem("tail_ve")
        tail_rs = sem("tail_rs")
        tail_h2 = sem("tail_h2")
        tail_turned = sem("tail_turned")
        tail_tT = sem("tail_tT")
        tail_gates = sem("tail_gates")
        tail_logged = sem("tail_logged")
        tail_out = sem("tail_out")
        tail_scattered = sem("tail_scattered")
        route_exp0 = sem("route_exp0")
        route_exp = sem("route_exp")
        onehot = sem("onehot")
        prefix_mm = sem("prefix_mm")
        routed = sem("routed")
        hs_in = [sem(f"hs_in{k}") for k in range(HS)]
        ext_ok = sem("ext_ok")
        scattered = [sem(f"scattered{k}") for k in range(HS)]
        we_in = [sem(f"we_in{k}") for k in range(NW)]
        xb_in = [sem(f"xb_in{k}") for k in range(NW)]
        xbT_mm = sem("xbT_mm")
        bT_done = sem("bT_done")
        hid_mm = [sem(f"hid_mm{m}") for m in range(4)]
        hid_done = [sem(f"hid_done{m}") for m in range(4)]
        y_mm = sem("y_mm")
        fin = sem("fin")
        y_done = sem("y_done")
        tok_ok = sem("tok_ok")
        out_done = [sem(f"out_done{k}") for k in range(2)]

        sp_passed, dve_passed, pool_passed = sem("sp_passed"), sem("dve_passed"), sem("pool_passed")

        block = keep.enter_context(nc.Block())

        def load_expert(eng, e, k):
            eng.dma_start(W1[:, k, :, :], w1_d[e].rearrange("(c p) n -> p c n", p=P)).then_inc(we_in[k], 16)
            eng.dma_start(W2[:, k, :, :], w2_d[e].rearrange("(m p) n -> p m n", p=P)).then_inc(we_in[k], 16)
            eng.dma_start(b1t[:, k, :], b1_d[e]).then_inc(we_in[k], 16)
            eng.dma_start(b2B[:, k, :], b2_d[e].unsqueeze(0).broadcast_to([P, D])).then_inc(we_in[k], 16)

        @block.sync
        def _(sp):
            start_counters(sp, [*post_out])
            sp.dma_start(cT[:, :], c_d).then_inc(mod_in, 16)
            sp.dma_start(wmod[:, 0:6 * D], wmod_d[0]).then_inc(mod_in, 16)
            sp.dma_start(wmod2[:, 0:6 * D], wmod_d[1]).then_inc(mod_in, 16)
            sp.dma_start(W[:, :], wqk_d[0]).then_inc(w_in, 16)
            sp.dma_start(Wv[:, :], wv_d[0]).then_inc(wv_in, 16)
            sp.dma_start(xw, x_d[0:TPB].rearrange("t p d -> p t d")).then_inc(xw_in, 16)
            sp.wait_ge(mod_rows, 6)
            sp.dma_start(mod_s, modr).then_inc(mod_out, 16)
            sp.wait_ge(mod_out, 16)
            sp.dma_start(modB[:, 0, :, :].rearrange("p k d -> p (k d)"),
                         mod_s[0:1, :].broadcast_to([P, 6 * D])).then_inc(modb0_in, 16)
            sp.dma_start(modB[:, 1:B, :, :].rearrange("p b k d -> p (b k d)"),
                         mod_s[1:B, :].rearrange("b n -> (b n)").unsqueeze(0).broadcast_to([P, (B - 1) * 6 * D])).then_inc(modb_in, 16)
            sp.dma_start(bvB[:, :], bv_d.broadcast_to([P, PAIRS * P])).then_inc(const_in, 16)
            sp.dma_start(boB[:, :], bo_d.broadcast_to([P, D])).then_inc(const_in, 16)
            sp.dma_start(wg[:, :, :], wg_d).then_inc(const_in, 16)
            sp.dma_start(bgB[:, :], bg_d.broadcast_to([P, NE])).then_inc(const_in, 16)
            sp.wait_ge(blank_set, 2)
            sp.wait_ge(wide_ss, 2)
            sp.dma_start(woT[:, :, :], wo_d).then_inc(wo_in, 16)

            def stack(st, kind, half):
                par = st.proj_par
                for name, count, use in ([("auxb", auxb_free, piece_use(st.pp, (kind, 0)))] * (half == 0 or kind == "q") +
                                         [("auxa", auxa_free, st.has("post") + piece_use(st.pp, (kind, 1)))] * half):
                    sp.wait_ge(count, st.of(name, use))
                    settle(sp, sp_passed)
                cols = slice(0, S) if kind == "q" else slice(half * HALF, (half + 1) * HALF)
                for h in range(2):
                    rows = slice(DH * h, DH * h + DH)
                    for part in range(2):
                        to = slice(DH * part, DH * part + DH)
                        if kind == "q":
                            move = sp.dma_start(QS[to, par, h, :].bitcast(F32), XQ[rows, part, :].bitcast(F32))
                        else:
                            move = sp.dma_start(KS[to, par, h, :, cols].bitcast(F32), XK[rows, :, cols].bitcast(F32))
                        move.then_inc(qk_in[par], 16)

            def load_tail(st):
                sp.wait_ge(s["wsplit"], st.of("wsplit", 1))
                sp.wait_ge(wv_split, B * COUPLES + 1)
                sp.wait_ge(s["hi"], st.n("hi"))
                sp.wait_ge(auxa_full, st.n("auxa"))
                sp.wait_ge(auxb_full, st.n("auxb"))
                sp.wait_ge(auxa_free, st.n("auxa"))
                sp.wait_ge(auxb_free, st.n("auxb"))
                b0, t0 = T0 // TPB, T0 % TPB
                sp.dma_start(zt[:, 1, :, :], z_s[b0 * PAIRS:(b0 + 1) * PAIRS, :, t0 * P:(t0 + 1) * P].rearrange("c p t -> p c t")).then_inc(tail_z0, 16)
                sp.dma_start(th[:, 0, D:2 * D], x_d[T0]).then_inc(tail_x, 16)
                sp.dma_start(th[:, 1:TAIL, D:2 * D], x_d[T0 + 1:NT].rearrange("t p d -> p t d")).then_inc(tail_x, 16)
                sp.dma_start(zA, z_s[NG - PAIRS:NG - 4].rearrange("c p t -> p c t")).then_inc(tail_z, 16)
                sp.wait_ge(z_out, 16 * (NG - 1))
                sp.dma_start(zB[:, 0:3, :], z_s[NG - 4:NG - 1].rearrange("c p t -> p c t")).then_inc(tail_z, 16)

            def step(st):
                g = st.g
                if st.has("post"):
                    t = st.tile
                    bt = t // TPB
                    tt = t % TPB
                    sp.wait_ge(z_out, 16 * (g - 1))
                    settle(sp, sp_passed)
                    sp.wait_ge(s["x1"], st.n("x1"))
                    settle(sp, sp_passed)
                    sp.dma_start(zt[:, st.pp, :, :],
                                 z_s[bass.ds(bt * PAIRS, PAIRS), :, bass.ds(tt * P, P)].rearrange("c p t -> p c t")).then_inc(zx_in[st.pp], 16)
                    sp.dma_start(xp[:, st.pp, :], x_d[t]).then_inc(zx_in[st.pp], 16)
                    if isinstance(st.b, int) and st.b == B:
                        load_tail(st)
                if st.has("proj"):
                    sp.wait_ge(s["wsplit"], st.of("wsplit", 1))
                    settle(sp, sp_passed)
                    sp.dma_start(W[:, :], wqk_d[(st.i + 1) % PAIRS]).then_inc(w_in, 16)
                    if st.pp == 0:
                        sp.wait_ge(wv_split, st.b * COUPLES + st.j + 1)
                        settle(sp, sp_passed)
                        sp.dma_start(Wv[:, :], wv_d[(st.j + 1) % COUPLES]).then_inc(wv_in, 16)
                if st.has("ln"):
                    sp.wait_ge(s["xn"], st.n("xn"))
                    settle(sp, sp_passed)
                    sp.dma_start(xln[:, st.pp, :], x_d[(st.b + 1) * TPB + st.i]).then_inc(xln_in[st.pp], 16)
                if st.has("proj"):
                    sp.wait_ge(scores_done[1], st.n("scores"))
                    settle(sp, sp_passed)
                    stack(st, "q", 1)
                    stack(st, "k", 0)
                if st.has("post"):
                    sp.wait_ge(s["x1"], st.of("x1", 1))
                    settle(sp, sp_passed)
                    sp.dma_start(xh_s[t][:, D:2 * D], x1[:, st.pp, :]).then_inc(post_out[st.pp], 16)
                    sp.dma_start(out_d[t], x1[:, st.pp, :]).then_inc(post_out[st.pp], 16)
                if st.has("proj"):
                    stack(st, "k", 1)
                    if st.b == 0:
                        for n in range(FILLS // PAIRS):
                            sp.dma_start(slots_s.rearrange("(k p i) w -> k p (i w)", p=P, i=FILL)[FILLS // PAIRS * st.i + n], blank).then_inc(filled, 16)
                    if isinstance(st.b, int) and st.b == 1 and isinstance(st.j, int):
                        sp.wait_ge(filled, 16 * FILLS)
                if st.has("post"):
                    sp.wait_ge(s["h2"], st.of("h2", 1))
                    settle(sp, sp_passed)
                    sp.dma_start(xh_s[t][:, 0:D], h2[:, st.pp, :]).then_inc(post_out[st.pp], 16)

            run_steps(sp, step)

            sp.wait_ge(s["pv"], TOTAL["pv"])
            sp.wait_ge(s["zevac"], TOTAL["zevac"])

            def load_slots(e, pp):
                sp.dma_start(xb[:, pp, :, :], slots_s[bass.ds(e * CAP, CAP), :].rearrange("(i p) d -> p i d", p=P)).then_inc(xb_in[pp], 16)

            for k in range(2):
                sp.wait_ge(post_out[k], 48 * ((T0 + 1 - k) // 2) + ONE)
            for k in range(HS):
                sp.dma_start(hs[:, k, 0:2 * D], xh_s[k]).then_inc(hs_in[k], 16)
            for k in range(2):
                load_expert(sp, k, k)
            sp.wait_ge(tail_h2, 1)
            sp.dma_start(xh_s[T0], th[:, 0, 0:2 * D]).then_inc(tail_out, 16)
            sp.dma_start(out_d[T0], th[:, 0, D:2 * D]).then_inc(tail_out, 16)
            sp.wait_ge(tail_out, 32)
            with sp.Fori(1, LOTS[-1][0] // HS) as j:
                for k in range(HS):
                    sp.wait_ge(scattered[k], 16 * j)
                    settle(sp, sp_passed)
                    sp.dma_start(hs[:, k, 0:2 * D], xh_s[HS * j + k]).then_inc(hs_in[k], 16)
            for k in range(2, NW):
                load_expert(sp, k, k)
            sp.wait_ge(tail_h2, len(GROUPS))
            sp.dma_start(out_d[T0 + 1:NT].rearrange("t p d -> p t d"), th[:, 1:TAIL, D:2 * D]).then_inc(tail_out, 16)
            for k in range(HS):
                sp.wait_ge(scattered[k], 16 * LOTS[-1][0] // HS)
            sp.wait_ge(tail_scattered, 16 * TPB)
            sp.wait_ge(tail_out, 48)
            for k in range(NW):
                load_slots(k, k)
            with sp.Fori(1, NE // NW) as j:
                for k in range(NW):
                    e = NW * j + k
                    sp.wait_ge(y_mm, e - NW + 1 + ONE)
                    settle(sp, sp_passed)
                    sp.wait_ge(y_done, e - NW + 1 + ONE)
                    settle(sp, sp_passed)
                    sp.wait_ge(tok_ok, e - NW + 1)
                    settle(sp, sp_passed)
                    load_slots(e, k)
                    load_expert(sp, e, k)

        @block.tensor
        def _(pe):
            start_counters(pe, [*scores_done, s["pv"], auxa_full, auxb_full, y_mm])
            pe.wait_ge(silu_done, 1)
            pe.wait_ge(mod_in, 48)
            banks = [XA, XB, Z]
            for k in range(3):
                for c, w in enumerate((wmod, wmod2)):
                    last = pe.matmul(banks[k][0:B, 0:HALF], sc[:, c * B:(c + 1) * B], w[:, k * HALF:(k + 1) * HALF],
                                     start=(c == 0), stop=(c == NC - 1))
            last.then_inc(mod_mm, 1)
            pe.wait_ge(mod_rows, 6)
            pe.wait_ge(consts, 5)
            for half in range(2):
                pe.wait_ge(wide_hn, half + 1)
                for c in range(NC):
                    for t in range(TPB // 2):
                        last = pe.transpose(SC[half][:, c * HALF + t * P:c * HALF + (t + 1) * P],
                                            hw[:, half * TPB // 2 + t, c * P:(c + 1) * P], ident[:, :])
                last.then_inc(wide_turned, 1)
            pe.wait_ge(wide_lo, 2)
            pe.wait_ge(const_in, 64)

            def step(st):
                g, pp, ap = st.g, st.pp, st.att_par
                used = {"a": 0, "b": 0}

                def aux(which):
                    bank, free, name = (XA, auxa_free, "auxa") if which == "a" else (XB, auxb_free, "auxb")
                    pe.wait_ge(free, st.of(name, used[which]))
                    used[which] += 1
                    return bank

                def project(kind, half):
                    bank = aux("b" if half % 2 == 0 else "a")
                    if kind == "q" and half == 0:
                        pe.wait_ge(s["wsplit"], st.of("wsplit", 1))
                        pe.wait_ge(auxa_free, st.n("auxa"))
                    if kind in "qk":
                        terms = ((Wh, hTh), (Wh, hTl), (Wl, hTh))
                        col = 0 if kind == "q" else P
                        for c in range(NC):
                            for n, (w, x) in enumerate(terms):
                                last = pe.matmul(bank[:, :], w[:, pp, c * QK + col:c * QK + col + P],
                                                 x[:, st.b % 2, c, half * HALF:(half + 1) * HALF],
                                                 start=(c == 0 and n == 0), stop=(c == NC - 1 and n == 2))
                    else:
                        if half == 0:
                            pe.wait_ge(wv_split, st.b * COUPLES + st.j + 1)
                        for t in range(2):
                            tok = (2 * half + t) * P
                            for c in range(NC):
                                for n, (w, x) in enumerate(((Wvh, hTh), (Wvl, hTh), (Wvh, hTl))):
                                    last = pe.matmul(bank[:, t * CV:(t + 1) * CV], x[:, st.b % 2, c, tok:tok + P],
                                                     w[:, c * CV:(c + 1) * CV],
                                                     start=(c == 0 and n == 0), stop=(c == NC - 1 and n == 2))
                    last.then_inc(auxb_full if half % 2 == 0 else auxa_full, 1)

                def score(kb, h):
                    pe.wait_ge(exp_done[h], st.of("expd", kb if kb <= 4 else kb - 1))
                    if kb == 0:
                        pe.wait_ge(qk_in[ap], qk_count(st))
                    lo = kb * P
                    spans = [(lo, HALF), (HALF, S)] if lo < HALF else [(lo, S)]
                    for a, z in spans:
                        at = a if kb < 4 else a - HALF + (kb % 2) * HALF
                        for part in range(2):
                            last = pe.matmul(SC[h][:, at:at + z - a], KS[:, ap, h, part, lo:lo + P],
                                             QS[:, ap, h, a:z], start=(part == 0), stop=(part == 1))
                    last.then_inc(scores_done[h], 1)

                def weigh(kb):
                    if kb == 0:
                        pe.wait_ge(s["zevac"], st.n("zevac"))
                    pe.wait_ge(s["vscaled"], st.of("vscaled", kb + 1))
                    lo = kb * P
                    spans = [(lo, HALF), (HALF, S)] if lo < HALF else [(lo, S)]
                    for a, z in spans:
                        for h in range(2):
                            last = pe.matmul(Z[DH * h:DH * h + DH, a:z], vs[:, kb % 2, DH * h:DH * h + DH],
                                             E[:, h, kb % 2, a:z], start=(kb == 0),
                                             stop=(kb == (3 if z == HALF else TPB - 1)))
                    last.then_inc(s["pv"], 1)

                def transpose_tile(x, which, ready):
                    bank = aux(which)
                    pe.wait_ge(s[ready], st.of(ready, 1))
                    for c in range(NC):
                        last = pe.transpose(bank[:, c * P:(c + 1) * P], x[:, c * P:(c + 1) * P], ident[:, :])
                    last.then_inc(auxa_full if which == "a" else auxb_full, 1)

                for kb in range(TPB):
                    if st.has("att"):
                        score(kb, 0)
                        score(kb, 1)
                        if kb >= 1:
                            weigh(kb - 1)
                    if st.has("post") and kb == 0:
                        if isinstance(st.b, int) and st.b == 1:
                            pe.wait_ge(wo_in, 16)
                        bank = aux("a")
                        pe.wait_ge(zx_in[pp], zx_count(st))
                        for c in range(PAIRS):
                            last = pe.matmul(bank[:, 0:D], zt[:, pp, c, :], woT[:, c, :], start=(c == 0), stop=(c == PAIRS - 1))
                        last.then_inc(auxa_full, 1)
                    if st.has("proj"):
                        for piece in PIECES[pp].get(kb, ()):
                            project(*piece)
                    if st.has("post") and kb == 6:
                        transpose_tile(h2[:, pp, :], "b", "h2")
                    if kb == 7:
                        if st.has("post"):
                            bank = aux("b")
                            for c in range(NC):
                                last = pe.matmul(bank[:, 0:NE], h2T[:, c, :], wg[:, c, :], start=(c == 0), stop=(c == NC - 1))
                            last.then_inc(auxb_full, 1)
                        if st.has("ln"):
                            transpose_tile(hn, "a", "hn")
                if st.has("att"):
                    weigh(TPB - 1)

            run_steps(pe, step)

            pe.wait_ge(auxa_free, TOTAL["auxa"])
            pe.wait_ge(auxb_free, TOTAL["auxb"])
            for h in range(2):
                pe.wait_ge(exp_done[h], TOTAL["expd"])
            pe.wait_ge(s["zevac"], TOTAL["zevac"])

            def project_out(n):
                u0, size = GROUPS[n]
                pe.wait_ge(*((tail_z0, 16) if n == 0 else (tail_z, 32)))
                for u in range(u0, u0 + size):
                    bank = Z[:, 0:D] if u == 0 else SC[(u - 1) // 4][:, (u - 1) % 4 * D:((u - 1) % 4 + 1) * D]
                    for c in range(PAIRS):
                        if u == 0:
                            z = zt[:, 1, c, :]
                        else:
                            z = [zA[:, c % 4, :], zB[:, c % 4, :]][c // 4] if c < PAIRS - 1 else zs
                            z = z[:, (u - 1) * P:u * P]
                        last = pe.matmul(bank, z, woT[:, c, :], start=(c == 0), stop=(c == PAIRS - 1))
                last.then_inc(tail_wo, 1)

            def gate_logits(n):
                u0, size = GROUPS[n]
                pe.wait_ge(tail_h2, n + 1)
                for q in range(size):
                    for c in range(NC):
                        last = pe.transpose(Z[:, (q * NC + c) * P:(q * NC + c + 1) * P],
                                            th[:, u0 + q, c * P:(c + 1) * P], ident[:, :])
                last.then_inc(tail_turned, 1)
                pe.wait_ge(tail_tT, n + 1)
                if n > 0:
                    pe.wait_ge(tail_logged, n)
                for q in range(size):
                    for c in range(NC):
                        at = HALF + (u0 + q) * NE
                        last = pe.matmul(Z[:, at:at + NE], tT[:, q * NC + c, :], wg[:, c, :], start=(c == 0), stop=(c == NC - 1))
                last.then_inc(tail_gates, 1)

            def ranks(lot):
                t0, t1 = LOTS[lot]
                if lot > 0:
                    pe.wait_ge(routed, lot)
                pe.wait_ge(onehot, lot + 1)
                pe.wait_ge(moe_const, 6)
                flat = oh[:, t0:t1, :].rearrange("p t e -> p (t e)")
                pe.matmul(XA[:, 0:(t1 - t0) * NE], tri[:, :], flat, start=True, stop=True)
                pe.matmul(XB[:, 0:(t1 - t0) * NE], ones[:, :], flat, start=True, stop=True).then_inc(prefix_mm, 1)

            ranks(0)
            project_out(0)
            project_out(1)
            project_out(2)
            gate_logits(0)
            project_out(3)
            gate_logits(1)
            ranks(1)
            project_out(4)
            gate_logits(2)
            gate_logits(3)
            gate_logits(4)
            ranks(2)
            pe.wait_ge(routed, len(LOTS))

            xbT = [XA, XB]
            hid = [SC[0][:, 0:HALF], SC[0][:, HALF:S], SC[1][:, 0:HALF], SC[1][:, HALF:S]]
            yps = [Z[:, 0:HALF], Z[:, HALF:S]]

            def hidden(e, j, k):
                pe.wait_ge(we_in[k], 64 * (j + 1))
                pe.wait_ge(bT_done, e + 1)
                for m in range(4):
                    if not isinstance(e, int) or e > 0:
                        pe.wait_ge(hid_done[m], e)
                    for half in range(2):
                        for c in range(NC):
                            col = (2 * m + half) * P
                            last = pe.matmul(hid[m][:, half * CAP:(half + 1) * CAP], W1[:, k, c, col:col + P],
                                             bT[:, k % 2, c, :], start=(c == 0), stop=(c == NC - 1))
                    last.then_inc(hid_mm[m], 1)

            def transpose_rows(e, j, k):
                if not isinstance(e, int) or e > 1:
                    pe.wait_ge(bT_done, e - 1)
                pe.wait_ge(xb_in[k], 16 * (j + 1))
                for c in range(NC):
                    for i in range(2):
                        last = pe.transpose(xbT[k % 2][:, c * CAP + i * P:c * CAP + (i + 1) * P],
                                            xb[:, k, i, c * P:(c + 1) * P], ident[:, :])
                last.then_inc(xbT_mm, 1)

            def expert(j, k):
                e = NW * j + k
                if not isinstance(e, int) or e + 1 < NE:
                    hidden(e + 1, j + (k + 1) // NW, (k + 1) % NW)
                if not isinstance(e, int) or e + 2 < NE:
                    transpose_rows(e + 2, j + (k + 2) // NW, (k + 2) % NW)
                pe.wait_ge(y_done, e + ONE)
                for m in range(4):
                    pe.wait_ge(hid_done[m], e + 1)
                for i in range(2):
                    for m in range(NM):
                        last = pe.matmul(yps[k % 2][:, i * D:(i + 1) * D], hh[:, k % 2, m, i * P:(i + 1) * P], W2[:, k, m, :],
                                         start=(m == 0), stop=(m == NM - 1))
                last.then_inc(y_mm, 1)

            transpose_rows(0, 0, 0)
            transpose_rows(1, 0, 1)
            hidden(0, 0, 0)
            run_experts(pe, expert)

        @block.scalar
        def _(act):
            start_counters(act, [*exp_done, auxb_free, s["zevac"], s["hi"], s["ss"], s["hThi"]])
            act.wait_ge(mod_in, 48)
            act.activation(ec[:, :], cT[:, :], ACT.Exp, scale=-1.0).then_inc(c_exp, 1)
            for half in range(2):
                act.wait_ge(wide_h, half + 1)
                for t in range(half * TPB // 2, (half + 1) * TPB // 2):
                    last = act.activation(xw[:, t, :], hw[:, t, :], ACT.Square, accum_out=wss[:, t:t + 1])
                last.then_inc(wide_ss, 1)
            for half in range(2):
                act.wait_ge(wide_turned, half + 1)
                act.activation(hTh[:, 0, :, half * HALF:(half + 1) * HALF], SC[half][:, :].rearrange("p (c t) -> p c t", c=NC),
                               ACT.Copy).then_inc(wide_hi, 1)

            def step(st):
                pp, ap = st.pp, st.att_par
                for kb in range(TPB):
                    if st.has("att"):
                        lo = kb * P
                        at = lo if kb < 4 else lo - HALF + (kb % 2) * HALF
                        for h in range(2):
                            if h == 0:
                                act.wait_ge(s["pv"], st.of("pv", kb - 1 if kb else 0))
                            act.wait_ge(negmax_done[h], st.of("negmax", kb + 1))
                            act.activation(E[:, h, kb % 2, lo:S], SC[h][:, at:at + S - lo], ACT.Exp,
                                           bias=nm[:, h, kb:kb + 1], scale=-1.0,
                                           accum_out=rs[:, kb, h:h + 1]).then_inc(exp_done[h], 1)
                    if st.has("ln") and kb == 3:
                        act.wait_ge(s["h"], st.of("h", 1))
                        act.activation(xnb[:, :], ha[:, :], ACT.Square, accum_out=lss[:, :]).then_inc(s["ss"], 1)
                    for kind, half in PIECES[pp].get(kb, ()) if st.has("proj") else ():
                        if kind == "v":
                            continue
                        use = piece_use(pp, (kind, half))
                        bank, full, at_ = ((XB, auxb_full, st.of("auxb", use)) if half == 0 else
                                           (XA, auxa_full, st.of("auxa", st.has("post") + use)))
                        act.wait_ge(full, at_)
                        if kind == "q" and half == 0:
                            act.wait_ge(s["wsplit"], st.of("wsplit", 1))
                            act.wait_ge(qk_in[1 - pp], qk_count(st))
                        x, k = (XQ, 0) if kind == "q" else (XK, 1)
                        act.activation(x[:, 0, half * HALF:(half + 1) * HALF], bank[:, :], ACT.Identity,
                                       bias=qkb[:, pp, k:k + 1], scale=-1.0 if k else 1.0).then_inc(s["hi"], 1)
                    if st.has("post") and kb == 6:
                        act.wait_ge(auxb_full, st.of("auxb", 3 * st.has("proj") + 1))
                        act.activation(h2T[:, :, :], XB[:, 0:D].rearrange("p (c t) -> p c t", c=NC), ACT.Copy).then_inc(auxb_free, 1)
                    if st.has("ln") and kb == 7:
                        act.wait_ge(auxa_full, st.of("auxa", st.has("post") + 3 * st.has("proj") + 1))
                        act.activation(hTh[:, (st.b + 1) % 2, :, bass.ds(st.i * P, P)],
                                       XA[:, 0:D].rearrange("p (c t) -> p c t", c=NC), ACT.Copy).then_inc(s["hThi"], 1)
                if st.has("att"):
                    act.wait_ge(s["pv"], st.of("pv", TPB))
                    act.wait_ge(z_out, 16 * st.g)
                    act.activation(zs[:, :], Z[:, :], ACT.Copy).then_inc(s["zevac"], 1)
                    act.wait_ge(s["zevac"], st.of("zevac", 1))
                    if not (isinstance(st.b, int) and st.b == B):
                        act.dma_start(z_s[st.g], zs[:, :]).then_inc(z_out, 16)

            run_steps(act, step)

            def turned(n):
                act.wait_ge(tail_turned, n + 1)
                size = GROUPS[n][1] * NC
                act.activation(tT[:, 0:size, :], Z[:, 0:size * P].rearrange("p (c t) -> p c t", c=size), ACT.Copy).then_inc(tail_tT, 1)

            def lot_exp(lot):
                t0, t1 = LOTS[lot]
                act.wait_ge(route_exp0, lot + 1)
                act.activation(rb[:, t0:t1, :], ra[:, t0:t1, :], ACT.Exp).then_inc(route_exp, 1)

            lot_exp(0)
            turned(0)
            lot_exp(1)
            for n in range(1, len(GROUPS)):
                turned(n)
            lot_exp(2)
            hid = [SC[0][:, 0:HALF], SC[0][:, HALF:S], SC[1][:, 0:HALF], SC[1][:, HALF:S]]
            xbT = [XA, XB]

            def rows(e, k):
                act.wait_ge(xbT_mm, e + 1)
                act.activation(bT[:, k % 2, :, :], xbT[k % 2][:, :].rearrange("p (c t) -> p c t", c=NC), ACT.Copy).then_inc(bT_done, 1)

            def hidden(e, k):
                if not isinstance(e, int) or e > 1:
                    act.wait_ge(y_mm, e - 1 + ONE)
                for m in (0, 2):
                    act.wait_ge(hid_mm[m], e + 1)
                    for half in range(2):
                        last = act.activation(hh[:, k % 2, 2 * m + half, :], hid[m][:, half * CAP:(half + 1) * CAP], ACT.Relu,
                                              bias=b1t[:, k, 2 * m + half:2 * m + half + 1])
                    last.then_inc(hid_done[m], 1)

            def expert(j, k):
                e = NW * j + k
                if not isinstance(e, int) or e + 1 < NE:
                    hidden(e + 1, (k + 1) % NW)
                if not isinstance(e, int) or e + 2 < NE:
                    rows(e + 2, (k + 2) % NW)

            rows(0, 0)
            rows(1, 1)
            hidden(0, 0)
            run_experts(act, expert)

        @block.vector
        def _(dve):
            start_counters(dve, [*negmax_done, auxa_free, y_done])
            start_counters(dve, [s[n] for n in ("vscaled", "rowinv", "xn", "lnve", "ms", "hn", "pve", "xn2", "dlink")])
            dve.wait_ge(c_exp, 1)
            dve.tensor_scalar(ec[:, :], ec[:, :], 1.0, None, ALU.add).then_inc(setup, 1)
            dve.wait_ge(setup, 1)
            dve.reciprocal(sc[:, :], ec[:, :]).then_inc(setup, 1)
            dve.wait_ge(setup, 2)
            dve.tensor_tensor(sc[:, :], sc[:, :], cT[:, :], ALU.mult).then_inc(silu_done, 1)
            dve.memset(mhalf[:, :], -0.5).then_inc(consts, 1)
            dve.wait_ge(mod_mm, 1)
            for k in range(6):
                src = [XA, XB, Z][k // 2][0:B, (k % 2) * D:(k % 2 + 1) * D]
                dst = modr[:, k * D:(k + 1) * D]
                if k in (SA, SB):
                    dve.tensor_copy(dst, src).then_inc(mod_rows, 1)
                elif k in (CA, CB):
                    dve.tensor_scalar(dst, src, 1.0, None, ALU.add).then_inc(mod_rows, 1)
                else:
                    n = 2 + 4 * (k == GB)
                    dve.wait_ge(mod_rows, k)
                    dve.tensor_scalar(sgn[:, 0, :], src, 0.0, 2.0, ALU.is_ge, ALU.mult).then_inc(setup, 1)
                    dve.wait_ge(setup, n + 1)
                    dve.tensor_scalar(sgn[:, 0, :], sgn[:, 0, :], -1.0, None, ALU.add).then_inc(setup, 1)
                    dve.tensor_scalar(sgn[:, 1, :], src, -1.0, 0.25, ALU.mult, ALU.max).then_inc(setup, 1)
                    dve.wait_ge(setup, n + 3)
                    dve.scalar_tensor_tensor(sgn[:, 1, :], src, 0.25, sgn[:, 1, :], ALU.max, ALU.max).then_inc(setup, 1)
                    dve.wait_ge(setup, n + 4)
                    dve.tensor_tensor(dst, sgn[:, 0, :], sgn[:, 1, :], ALU.mult).then_inc(mod_rows, 1)

            dve.wait_ge(xw_in, 16)
            for t in range(TPB):
                dve.bn_stats(wst[:, t, :], xw[:, t, :]).then_inc(wide, 1)
            for t in range(TPB):
                dve.wait_ge(wide, t + 1)
                dve.bn_aggr(wmv[:, t, :], wst[:, t, :]).then_inc(wide, 1)
            dve.wait_ge(wide, 2 * TPB)
            dve.tensor_scalar(wve, wmv[:, :, 1], LN_EPS, None, ALU.add).then_inc(wide_ve, 1)
            dve.wait_ge(wide_rs, 1)
            dve.wait_ge(mod_out, 16)
            for t in range(TPB):
                dve.tensor_scalar(hw[:, t, :], xw[:, t, :], wmv[:, t, 0:1], wrs[:, t:t + 1], ALU.subtract, ALU.mult).then_inc(wide, 1)
            dve.wait_ge(modb0_in, 16)
            halves = [slice(0, TPB // 2), slice(TPB // 2, TPB)]
            for half, tiles in enumerate(halves):
                dve.wait_ge(wide, 2 * TPB + (half + 1) * TPB // 2 + half)
                dve.tensor_tensor(hw[:, tiles, :], hw[:, tiles, :], modB[:, 0, CA, :].unsqueeze(1).broadcast_to([P, TPB // 2, D]),
                                  ALU.mult).then_inc(wide, 1)
                dve.wait_ge(wide, 3 * TPB + half + 1)
                dve.tensor_tensor(hw[:, tiles, :], hw[:, tiles, :], modB[:, 0, SA, :].unsqueeze(1).broadcast_to([P, TPB // 2, D]),
                                  ALU.add).then_inc(wide_h, 1)
            for half, tiles in enumerate(halves):
                dve.wait_ge(wide_ss, half + 1)
                dve.tensor_scalar(wms[:, tiles], wss[:, tiles], 1.0 / D, RMS_EPS, ALU.mult, ALU.add).then_inc(wide_ms, 1)
            for half in range(2):
                dve.wait_ge(wide_rr, half + 1)
                for t in range(half * TPB // 2, (half + 1) * TPB // 2):
                    last = dve.tensor_scalar(hw[:, t, :], hw[:, t, :], wrr[:, t:t + 1], None, ALU.mult)
                last.then_inc(wide_hn, 1)
            for half in range(2):
                cols = slice(half * HALF, (half + 1) * HALF)
                dve.wait_ge(wide_hi, half + 1)
                dve.tensor_tensor(hTl[:, 0, :, cols], SC[half][:, :].rearrange("p (c t) -> p c t", c=NC),
                                  hTh[:, 0, :, cols].bitcast(F32), ALU.subtract).then_inc(wide_lo, 1)

            dve.wait_ge(consts, 5)
            dve.wait_ge(const_in, 64)

            def step(st):
                pp, ap = st.pp, st.att_par
                links = [0]

                def link(ins):
                    links[0] += 1
                    ins.then_inc(s["dlink"], 1)
                    dve.wait_ge(s["dlink"], st.of("dlink", links[0]))

                def stats(x, stt, mv, ve):
                    link(dve.bn_stats(stt[:, :], x))
                    settle(dve, dve_passed)
                    link(dve.bn_aggr(mv[:, :], stt[:, :]))
                    return dve.tensor_scalar(ve[:, :], mv[:, 1:2], LN_EPS, None, ALU.add)

                def scale_values(kb):
                    if kb == 0:
                        dve.wait_ge(auxa_free, st.n("auxa"))
                        dve.wait_ge(auxb_free, st.n("auxb"))
                    if st.has("proj") and pp == 1 and kb in (4, 6):
                        full, name = (auxb_free, "auxb") if kb == 4 else (auxa_free, "auxa")
                        use = piece_use(pp, ("v", kb // 2)) + (st.has("post") if kb == 6 else 0)
                        dve.wait_ge(full, st.of(name, use))
                    for h in range(2):
                        dve.wait_ge(exp_done[h], st.of("expd", kb + 1))
                    dve.reciprocal(ri[:, kb % 2, :], rs[:, kb, :]).then_inc(s["rowinv"], 1)
                    if kb >= 2:
                        dve.wait_ge(s["pv"], st.of("pv", kb - 1))
                    else:
                        dve.wait_ge(s["pv"], st.n("pv"))
                    dve.wait_ge(s["rowinv"], st.of("rowinv", kb + 1))
                    dve.tensor_tensor(vs[:, kb % 2, :].rearrange("p (h d) -> p h d", h=2),
                                      V[:, kb, ap, :].rearrange("p (h d) -> p h d", h=2),
                                      ri[:, kb % 2, :].unsqueeze(2).broadcast_to([P, 2, DH]), ALU.mult).then_inc(s["vscaled"], 1)

                for kb in range(TPB):
                    if st.has("att"):
                        lo = kb * P
                        at = lo if kb < 4 else lo - HALF + (kb % 2) * HALF
                        for h in range(2):
                            dve.wait_ge(scores_done[h], st.of("scores", kb + 1))
                            settle(dve, dve_passed)
                            dve.tensor_tensor_reduce(SC[h][:, at:at + S - lo], SC[h][:, at:at + S - lo], mask[:, 0:S - lo],
                                                     1.0, BIG, ALU.add, ALU.min, nm[:, h, kb:kb + 1]).then_inc(negmax_done[h], 1)
                    if st.has("post") and kb == 1:
                        dve.wait_ge(auxa_full, st.of("auxa", 1))
                        dve.wait_ge(s["x1"], st.n("x1"))
                        dve.tensor_tensor(pt[:, :], XA[:, 0:D], boB[:, :], ALU.add).then_inc(auxa_free, 1)
                    for kind, half in PIECES[pp].get(kb - 1, ()) if st.has("proj") else ():
                        use = piece_use(pp, (kind, half))
                        cols = slice(half * HALF, (half + 1) * HALF)
                        bank, free, full, at_ = ((XB, auxb_free, auxb_full, st.of("auxb", use)) if half % 2 == 0 else
                                                 (XA, auxa_free, auxa_full, st.of("auxa", st.has("post") + use)))
                        if kind == "v":
                            dve.wait_ge(full, at_)
                            last = dve.tensor_tensor(V[:, 2 * half:2 * half + 2, :, :].rearrange("p t a d -> p t (a d)"),
                                                     bank[:, :].rearrange("p (t d) -> p t d", t=2),
                                                     bvB[:, bass.ds(st.j * CV, CV)].unsqueeze(1).broadcast_to([P, 2, CV]), ALU.add)
                        else:
                            order = [p for k in sorted(PIECES[pp]) for p in PIECES[pp][k] if p[0] != "v"]
                            dve.wait_ge(s["hi"], st.of("hi", order.index((kind, half)) + 1))
                            if kind == "q":
                                last = dve.scalar_tensor_tensor(XQ[:, 1, cols], bank[:, :], qkb[:, pp, 0:1],
                                                                XQ[:, 0, cols].bitcast(F32), ALU.add, ALU.subtract)
                            else:
                                last = dve.scalar_tensor_tensor(XK[:, 1, cols], bank[:, :], qkb[:, pp, 1:2],
                                                                XK[:, 0, cols].bitcast(F32), ALU.subtract, ALU.subtract,
                                                                reverse0=True)
                        last.then_inc(free, 1)
                    if st.has("ln"):
                        if kb == 0:
                            dve.wait_ge(xln_in[pp], 16 * (st.b * PAIRS // 2 + st.j + 1))
                            stats(xln[:, pp, :], lst, lmv, lve).then_inc(s["lnve"], 1)
                        if kb == 1:
                            dve.wait_ge(s["rstd"], st.of("rstd", 1))
                            dve.wait_ge(s["h"], st.n("h"))
                            dve.tensor_scalar(xnb[:, :], xln[:, pp, :], lmv[:, 0:1], lrs[:, :], ALU.subtract,
                                              ALU.mult).then_inc(s["xn"], 1)
                        if kb == 4:
                            dve.wait_ge(s["ss"], st.of("ss", 1))
                            dve.tensor_scalar(lms[:, :], lss[:, :], 1.0 / D, RMS_EPS, ALU.mult, ALU.add).then_inc(s["ms"], 1)
                        if kb == 6:
                            dve.wait_ge(s["rr"], st.of("rr", 1))
                            dve.wait_ge(auxa_full, st.n("auxa"))
                            dve.tensor_scalar(hn[:, :], ha[:, :], lrr[:, :], None, ALU.mult).then_inc(s["hn"], 1)
                    if st.has("post"):
                        if kb == 2:
                            dve.wait_ge(s["x1"], st.of("x1", 1))
                            stats(x1[:, pp, :], pst, pmv, pve).then_inc(s["pve"], 1)
                        if kb == 3:
                            dve.wait_ge(s["prstd"], st.of("prstd", 1))
                            dve.wait_ge(s["h2"], st.n("h2"))
                            dve.tensor_scalar(xn2[:, :], x1[:, pp, :], pmv[:, 0:1], prs[:, :], ALU.subtract,
                                              ALU.mult).then_inc(s["xn2"], 1)
                    if st.has("att"):
                        scale_values(kb)
                if st.has("post"):
                    dve.wait_ge(auxb_full, st.of("auxb", 3 * st.has("proj") + 2))
                    dve.tensor_tensor(logits[:, bass.ds(st.tile, 1), :], XB[:, 0:NE].unsqueeze(1), bgB[:, :].unsqueeze(1), ALU.add)\
                        .then_inc(auxb_free, 1)
                if st.has("ln"):
                    dve.wait_ge(s["hThi"], st.of("hThi", 1))
                    cols = bass.ds(st.i * P, P)
                    dve.tensor_tensor(hTl[:, (st.b + 1) % 2, :, cols], XA[:, 0:D].rearrange("p (c t) -> p c t", c=NC),
                                      hTh[:, (st.b + 1) % 2, :, cols].bitcast(F32), ALU.subtract).then_inc(auxa_free, 1)
                assert links[0] == sum(v for k, v in RISES["dlink"].items() if st.has(k))

            run_steps(dve, step)

            steps = [0]

            def link(ins):
                steps[0] += 1
                ins.then_inc(route, 1)
                dve.wait_ge(route, steps[0])

            def norm_tail(n):
                u0, size = GROUPS[n]
                tiles = slice(u0, u0 + size)
                b = (T0 + u0) // TPB

                def each(row):
                    return row.unsqueeze(1).broadcast_to([P, size, D])

                x1_, h2_, rows = th[:, tiles, D:2 * D], th[:, tiles, 0:D], tp[:, 0:size, :]
                bank = Z[:, 0:D] if u0 == 0 else SC[(u0 - 1) // 4][:, (u0 - 1) % 4 * D:((u0 - 1) % 4 + size) * D]
                dve.wait_ge(tail_wo, n + 1)
                link(dve.tensor_tensor(rows, bank.rearrange("p (q d) -> p q d", q=size), each(boB[:, :]), ALU.add))
                link(dve.tensor_tensor(rows, rows, each(modB[:, b, GA, :]), ALU.mult))
                dve.wait_ge(tail_x, 32)
                link(dve.tensor_tensor(x1_, rows, x1_, ALU.add))
                for q in range(size):
                    link(dve.bn_stats(tst[:, q, :], th[:, u0 + q, D:2 * D]))
                for q in range(size):
                    link(dve.bn_aggr(tmv[:, q, :], tst[:, q, :]))
                dve.tensor_scalar(tve[:, 0:size], tmv[:, 0:size, 1], LN_EPS, None, ALU.add).then_inc(tail_ve, 1)
                dve.wait_ge(tail_rs, n + 1)
                for q in range(size):
                    link(dve.tensor_scalar(th[:, u0 + q, 0:D], th[:, u0 + q, D:2 * D], tmv[:, q, 0:1], trs[:, q:q + 1],
                                           ALU.subtract, ALU.mult))
                link(dve.tensor_tensor(h2_, h2_, each(modB[:, b, CB, :]), ALU.mult))
                dve.tensor_tensor(h2_, h2_, each(modB[:, b, SB, :]), ALU.add).then_inc(tail_h2, 1)

            def tail_logits(n):
                u0, size = GROUPS[n]
                dve.wait_ge(tail_gates, n + 1)
                at = HALF + u0 * NE
                dve.tensor_tensor(logits[:, T0 + u0:T0 + u0 + size, :],
                                  Z[:, at:at + size * NE].rearrange("p (q e) -> p q e", q=size),
                                  bgB[:, :].unsqueeze(1).broadcast_to([P, size, NE]), ALU.add).then_inc(tail_logged, 1)

            def route_lot(lot):
                t0, t1 = LOTS[lot]
                tiles, count = slice(t0, t1), t1 - t0

                def wide(a):
                    return a[:, tiles].unsqueeze(2).broadcast_to([P, count, NE])

                def each(a):
                    return a.unsqueeze(1).broadcast_to([P, count, NE])

                ra_, rb_, rc_, oh_ = (x[:, tiles, :] for x in (ra, rb, rc, oh))
                link(dve.tensor_reduce(r1[:, tiles], logits[:, tiles, :], AX.X, ALU.max))
                dve.tensor_tensor(ra_, logits[:, tiles, :], wide(r1), ALU.subtract).then_inc(route_exp0, 1)
                dve.wait_ge(route_exp0, lot + 1)
                link(dve.tensor_scalar(rc_, ra_, 0.0, None, ALU.is_ge))
                link(dve.tensor_tensor(rc_, rc_, each(revj[:, :]), ALU.mult))
                link(dve.tensor_reduce(r2[:, tiles], rc_, AX.X, ALU.max))
                dve.tensor_tensor(oh_, rc_, wide(r2), ALU.is_equal).then_inc(onehot, 1)
                dve.wait_ge(route_exp, lot + 1)
                link(dve.tensor_reduce(r3[:, tiles], rb_, AX.X, ALU.add))
                link(dve.reciprocal(r3[:, tiles], r3[:, tiles]))
                dve.wait_ge(onehot, lot + 1)
                link(dve.tensor_tensor(rc_, oh_, each(ebase[:, :]), ALU.mult))
                link(dve.tensor_reduce(r4[:, tiles], rc_, AX.X, ALU.add))
                if t0 == 0:
                    link(dve.memset(base[:, 0, :], 0.0))
                dve.wait_ge(prefix_mm, lot + 1)
                tot = XB[:, 0:count * NE].rearrange("p (t e) -> p t e", t=count)
                for t in range(t0 + 1, min(t1 + 1, NT)):
                    link(dve.tensor_tensor(base[:, t, :], base[:, t - 1, :], tot[:, t - 1 - t0, :], ALU.add))
                link(dve.tensor_tensor(ra_, XA[:, 0:count * NE].rearrange("p (t e) -> p t e", t=count), base[:, tiles, :], ALU.add))
                link(dve.tensor_tensor(ra_, ra_, oh_, ALU.mult))
                link(dve.tensor_reduce(r1[:, tiles], ra_, AX.X, ALU.add))
                link(dve.tensor_scalar(keepm[:, tiles], r1[:, tiles], float(CAP), None, ALU.is_lt))
                link(dve.tensor_tensor(gates[:, tiles], r3[:, tiles], keepm[:, tiles], ALU.mult))
                link(dve.tensor_tensor(r1[:, tiles], r1[:, tiles], r4[:, tiles], ALU.add))
                link(dve.tensor_scalar(r2[:, tiles], keepm[:, tiles], -FAR, FAR, ALU.mult, ALU.add))
                link(dve.tensor_tensor(slot_u[:, tiles], r1[:, tiles], r2[:, tiles], ALU.add))
                for b in range(t0 // TPB, t1 // TPB):
                    part = slice(b * TPB, (b + 1) * TPB)
                    last = dve.tensor_copy(ext[:, part, 1 + b:2 + b], gates[:, part].unsqueeze(2))
                    if b + 1 < t1 // TPB or t1 == NT:
                        link(last)
                if t1 == NT:
                    last = dve.tensor_copy(th[:, 1:TAIL, 2 * D:ROW], ext[:, tiles, :])
                last.then_inc(routed, 1)

            dve.wait_ge(moe_const, 6)
            dve.wait_ge(auxb_free, TOTAL["auxb"])
            dve.wait_ge(s["pv"], TOTAL["pv"])
            route_lot(0)
            norm_tail(0)
            norm_tail(1)
            tail_logits(0)
            dve.wait_ge(tail_logged, 1)
            route_lot(1)
            for n in range(2, len(GROUPS)):
                norm_tail(n)
                tail_logits(n - 1)
            tail_logits(len(GROUPS) - 1)
            dve.wait_ge(tail_logged, len(GROUPS))
            route_lot(2)

            hid = [SC[0][:, 0:HALF], SC[0][:, HALF:S], SC[1][:, 0:HALF], SC[1][:, HALF:S]]

            def hidden(e, k):
                if not isinstance(e, int) or e > 1:
                    dve.wait_ge(y_mm, e - 1 + ONE)
                for m in (1, 3):
                    dve.wait_ge(hid_mm[m], e + 1)
                    for half in range(2):
                        last = dve.tensor_scalar(hh[:, k % 2, 2 * m + half, :], hid[m][:, half * CAP:(half + 1) * CAP],
                                                 b1t[:, k, 2 * m + half:2 * m + half + 1], 0.0, ALU.add, ALU.max)
                    last.then_inc(hid_done[m], 1)

            FIN = 2 * B + 2

            def expert(j, k):
                e = NW * j + k
                if not isinstance(e, int) or e + 1 < NE:
                    hidden(e + 1, (k + 1) % NW)
                dve.wait_ge(xb_in[k], 16 * (j + 1))
                for b in range(B):
                    for i in range(2):
                        col = xb[:, k, i, GATE + b:GATE + b + 1]
                        if b == 0:
                            if not isinstance(e, int) or e > 0:
                                dve.wait_ge(fin, FIN * e)
                            last = dve.tensor_scalar(grow[:, i, :], modB[:, b, GB, :], col, None, ALU.mult)
                        else:
                            dve.wait_ge(fin, FIN * e + 2 * (b - 1) + i + 1)
                            last = dve.scalar_tensor_tensor(grow[:, i, :], modB[:, b, GB, :], col, grow[:, i, :],
                                                            ALU.mult, ALU.add)
                        last.then_inc(fin, 1)
                dve.wait_ge(y_mm, e + 1 + ONE)
                if not isinstance(e, int) or e > 1:
                    dve.wait_ge(out_done[k % 2], 32 * (NW // 2 * j + k // 2))
                rows = yb[:, k % 2, :, :]
                dve.tensor_tensor(rows, Z[:, (k % 2) * HALF:(k % 2 + 1) * HALF].rearrange("p (i d) -> p i d", i=2),
                                  b2B[:, k, :].unsqueeze(1).broadcast_to([P, 2, D]), ALU.add).then_inc(fin, 1)
                dve.wait_ge(fin, FIN * e + 2 * B + 1)
                dve.tensor_tensor(rows, rows, grow[:, :, :], ALU.mult).then_inc(fin, 1)
                dve.wait_ge(fin, FIN * e + 2 * B + 2)
                dve.tensor_tensor(rows, rows, xb[:, k, :, D:2 * D], ALU.add).then_inc(y_done, 1)

            hidden(0, 0)
            run_experts(dve, expert)

        @block.gpsimd
        def _(pool):
            start_counters(pool, [s[n] for n in ("rstd", "h", "rr", "x1", "prstd", "h2", "plink", "wsplit")])
            pool.memset(ident[:, :], 0.0).then_inc(consts, 1)
            pool.memset(mask[:, :], 0.0).then_inc(consts, 1)
            pool.wait_ge(consts, 3)
            pool.affine_select(ident[:, :], ident[:, :], pattern=[[-1, P]], compare_op=ALU.not_equal, fill=1.0,
                               base=0, channel_multiplier=1).then_inc(consts, 1)
            pool.affine_select(mask[:, 0:P], mask[:, 0:P], pattern=[[1, P]], compare_op=ALU.is_ge, fill=BIG,
                               base=0, channel_multiplier=-1).then_inc(consts, 1)
            pool.memset(blank, 0.0).then_inc(blank_set, 1)
            pool.wait_ge(blank_set, 1)
            pool.memset(blank.rearrange("p (i w) -> p i w", i=FILL)[:, :, TOKEN:TOKEN + 1], FAR).then_inc(blank_set, 1)

            def split_weights(par):
                pool.tensor_copy(qkb[:, par, 0:1], W[:, NC * QK:NC * QK + 1])
                pool.tensor_scalar(qkb[:, par, 1:2], W[:, NC * QK + 1:NC * QK + 2], -1.0, None, ALU.mult)
                return pool.tensor_copy(Wh[:, par, :], W[:, 0:NC * QK])

            def last_split(par):
                return pool.tensor_tensor(Wl[:, par, :], W[:, 0:NC * QK], Wh[:, par, :].bitcast(F32), ALU.subtract)

            def split_values_weights(n):
                pool.wait_ge(wv_in, 16 * n)
                settle(pool, pool_passed)
                pool.tensor_copy(Wvh[:, :], Wv[:, :]).then_inc(wv_lead, 1)
                pool.wait_ge(wv_lead, n)
                pool.tensor_tensor(Wvl[:, :], Wv[:, :], Wvh[:, :].bitcast(F32), ALU.subtract).then_inc(wv_split, 1)

            def step(st):
                pp = st.pp
                links = [0]

                def link(ins):
                    links[0] += 1
                    ins.then_inc(s["plink"], 1)
                    pool.wait_ge(s["plink"], st.of("plink", links[0]))

                if st.has("ln"):
                    pool.wait_ge(s["lnve"], st.of("lnve", 1))
                    pool.tensor_tensor(lrs[:, :], lve[:, :], mhalf[:, :], ALU.pow).then_inc(s["rstd"], 1)
                    pool.wait_ge(s["xn"], st.of("xn", 1))
                    pool.wait_ge(s["hn"], st.n("hn"))
                    link(pool.tensor_tensor(ha[:, :], xnb[:, :], modB[:, st.b + 1, CA, :], ALU.mult))
                    pool.tensor_tensor(ha[:, :], ha[:, :], modB[:, st.b + 1, SA, :], ALU.add).then_inc(s["h"], 1)
                if st.has("post"):
                    bt = st.tile // TPB
                    pool.wait_ge(auxa_free, st.of("auxa", 1))
                    link(pool.tensor_tensor(pt[:, :].unsqueeze(1), pt[:, :].unsqueeze(1), modB[:, bass.ds(bt, 1), GA, :], ALU.mult))
                    pool.wait_ge(zx_in[pp], zx_count(st))
                    pool.wait_ge(post_out[pp], (zx_count(st) - 32) // 2 * 3 + ONE)
                    pool.tensor_tensor(x1[:, pp, :], pt[:, :], xp[:, pp, :], ALU.add).then_inc(s["x1"], 1)
                    pool.wait_ge(s["pve"], st.of("pve", 1))
                    pool.tensor_tensor(prs[:, :], pve[:, :], mhalf[:, :], ALU.pow).then_inc(s["prstd"], 1)
                    pool.wait_ge(s["xn2"], st.of("xn2", 1))
                    link(pool.tensor_tensor(h2[:, pp, :].unsqueeze(1), xn2[:, :].unsqueeze(1), modB[:, bass.ds(bt, 1), CB, :], ALU.mult))
                    pool.tensor_tensor(h2[:, pp, :].unsqueeze(1), h2[:, pp, :].unsqueeze(1), modB[:, bass.ds(bt, 1), SB, :], ALU.add).then_inc(s["h2"], 1)
                if st.has("ln"):
                    pool.wait_ge(s["ms"], st.of("ms", 1))
                    pool.tensor_tensor(lrr[:, :], lms[:, :], mhalf[:, :], ALU.pow).then_inc(s["rr"], 1)
                if st.has("proj"):
                    pool.wait_ge(w_in, 16 * (st.b * PAIRS + st.i + 2))
                    pool.wait_ge(auxa_full, st.n("auxa"))
                    pool.wait_ge(auxb_full, st.n("auxb"))
                    settle(pool, pool_passed)
                    link(split_weights(1 - pp))
                    last_split(1 - pp).then_inc(s["wsplit"], 1)
                    if pp == 1:
                        pool.wait_ge(auxb_full, st.of("auxb", piece_use(pp, ("v", 2))))
                        pool.wait_ge(auxa_full, st.of("auxa", st.has("post") + piece_use(pp, ("v", 3))))
                        split_values_weights(st.b * COUPLES + st.j + 2)

            pool.wait_ge(w_in, 16)
            split_weights(0).then_inc(setup_split, 1)
            pool.wait_ge(setup_split, 1)
            last_split(0).then_inc(s["wsplit"], 1)
            split_values_weights(1)

            minus_halves = mhalf[:, :].broadcast_to([P, TPB])
            pool.wait_ge(consts, 5)
            pool.wait_ge(wide_ve, 1)
            pool.tensor_tensor(wrs, wve, minus_halves, ALU.pow).then_inc(wide_rs, 1)
            for half in range(2):
                tiles = slice(half * TPB // 2, (half + 1) * TPB // 2)
                pool.wait_ge(wide_ms, half + 1)
                pool.tensor_tensor(wrr[:, tiles], wms[:, tiles], minus_halves[:, tiles], ALU.pow).then_inc(wide_rr, 1)
            pool.wait_ge(modb_in, 16)

            run_steps(pool, step)

            pool.memset(ext[:, :, :], 0.0).then_inc(moe_const, 1)
            pool.memset(ones[:, :], 1.0).then_inc(moe_const, 1)
            pool.wait_ge(moe_const, 2)
            pool.affine_select(tri[:, :], ones[:, :], pattern=[[1, P]], compare_op=ALU.is_gt, fill=0.0,
                               base=0, channel_multiplier=-1).then_inc(moe_const, 1)
            pool.iota(revj[:, :], pattern=[[-1, NE]], base=NE, channel_multiplier=0,
                      allow_small_or_imprecise_dtypes=True).then_inc(moe_const, 1)
            pool.iota(ebase[:, :], pattern=[[CAP, NE]], base=0, channel_multiplier=0,
                      allow_small_or_imprecise_dtypes=True).then_inc(moe_const, 1)
            pool.iota(ext[:, :, 0:1], pattern=[[P, NT]], base=0, channel_multiplier=1,
                      allow_small_or_imprecise_dtypes=True).then_inc(moe_const, 1)

            def tail_pow(n, size=2):
                pool.wait_ge(tail_ve, n + 1)
                pool.tensor_tensor(trs[:, 0:size], tve[:, 0:size], mhalf[:, :].broadcast_to([P, size]), ALU.pow).then_inc(tail_rs, 1)

            tail_pow(0, 1)

            def scatter(j, parts=(0, 1)):
                for k0 in (part * HS // 2 for part in parts):
                    ks = range(k0, k0 + HS // 2)
                    if j > 0:
                        for k in ks:
                            pool.wait_ge(scattered[k], 16 * j)
                    pool.tensor_copy(hs[:, k0:k0 + HS // 2, 2 * D:ROW], ext[:, HS * j + k0:HS * j + k0 + HS // 2, :]).then_inc(ext_ok, 1)
                    pool.wait_ge(ext_ok, 2 * j + k0 // (HS // 2) + 1)
                    for k in ks:
                        t = HS * j + k
                        pool.wait_ge(hs_in[k], 16 * (j + 1))
                        pool.indirect_dma_start(slots_s, bass.IndirectOffsetOnAxis(slot_u[:, t:t + 1], 0), hs[:, k, :], None,
                                                bounds_check=NE * CAP - 1, oob_is_err=False).then_inc(scattered[k], 16)

            pool.wait_ge(filled, 16 * FILLS)
            pool.wait_ge(routed, 1)
            scatter(0)
            tail_pow(1)
            scatter(1)
            tail_pow(2)
            pool.wait_ge(routed, 2)
            scatter(2, (0,))
            tail_pow(3)
            scatter(2, (1,))
            tail_pow(4)
            pool.wait_ge(routed, 3)
            for k in range(TPB):
                pool.indirect_dma_start(slots_s, bass.IndirectOffsetOnAxis(slot_u[:, NT - TPB + k:NT - TPB + k + 1], 0), th[:, 1 + k, :], None,
                                        bounds_check=NE * CAP - 1, oob_is_err=False).then_inc(tail_scattered, 16)

            out_rows = out_d.rearrange("t p d -> (t p) d")

            def expert(j, k):
                e = NW * j + k
                pool.wait_ge(xb_in[k], 16 * (j + 1))
                if not isinstance(e, int) or e > 1:
                    pool.wait_ge(out_done[k % 2], 32 * (NW // 2 * j + k // 2))
                settle(pool, pool_passed)
                pool.tensor_copy(tok[:, k % 2, :].unsqueeze(2), xb[:, k, :, TOKEN:TOKEN + 1]).then_inc(tok_ok, 1)
                pool.wait_ge(tok_ok, e + 1)
                pool.wait_ge(y_done, e + 1 + ONE)
                settle(pool, pool_passed)
                for i in range(2):
                    pool.indirect_dma_start(out_rows, bass.IndirectOffsetOnAxis(tok[:, k % 2, i:i + 1], 0), yb[:, k % 2, i, :], None,
                                            bounds_check=NT * P - 1, oob_is_err=False).then_inc(out_done[k % 2], 16)

            run_experts(pool, expert)
            for k in range(2):
                pool.wait_ge(out_done[k], 32 * (NE // 2))


def kernel(**inputs):
    import numpy as np
    import concourse.bacc as bacc
    from concourse.bass_utils import run_bass_kernel_spmd

    a = {k: np.asarray(v) for k, v in inputs.items()}
    w = a["L0_attn_W_qkv"].reshape(PAIRS, 2, DH, 3, NC, P).transpose(0, 5, 4, 3, 1, 2).reshape(PAIRS, P, NC, 3, P)
    wqk = w[:, :, :, 0:2].reshape(PAIRS, P, NC * QK)
    wv = w[:, :, :, 2].reshape(COUPLES, 2, P, NC, P).transpose(0, 2, 3, 1, 4).reshape(COUPLES, P, NC * CV)
    bqkv = a["L0_attn_b_qkv"].reshape(PAIRS, P, 3)
    arrays = {
        "x": a["L0_attn_x"].reshape(NT, P, D),
        "wqk": np.concatenate([wqk, bqkv[:, :, 0:2]], axis=2),
        "wv": wv,
        "bv": bqkv[:, :, 2].reshape(1, PAIRS * P),
        "wo": a["L0_attn_W_o"].T.reshape(PAIRS, P, D).transpose(1, 0, 2),
        "bo": a["L0_attn_b_o"].reshape(1, D),
        "wg": a["L0_ffn_Wg"].reshape(NC, P, NE).transpose(1, 0, 2),
        "bg": a["L0_ffn_bg"].reshape(1, NE),
        "w1": a["L0_ffn_W1"],
        "b1": a["L0_ffn_b1"].reshape(NE, NM, P).transpose(0, 2, 1),
        "w2": a["L0_ffn_W2"],
        "b2": a["L0_ffn_b2"],
        "c": a["L0_c"].reshape(B, NC, P).transpose(2, 1, 0).reshape(P, NC * B),
        "wmod": a["L0_wmod"].reshape(NC, P, 6 * D),
    }
    nc = bacc.Bacc("TRN2", target_bir_lowering=False, num_devices=1)
    feeds, args = {}, []
    for name, v in arrays.items():
        v = np.ascontiguousarray(v)
        feeds[f"in_{name}"] = v
        args.append(nc.dram_tensor(f"in_{name}", v.shape, mybir.dt.from_np(v.dtype), kind="ExternalInput").ap())
    args.append(nc.dram_tensor("out", [NT, P, D], F32, kind="ExternalOutput").ap())
    adaln_block(nc, *args)
    r = run_bass_kernel_spmd(nc, [feeds], core_ids=[0])
    return r.results[0]["out"].reshape(B, S, D)
```
